# Optimizing a Trainium2 kernel written in Bass

```python
import numpy as np
import jax
import jax.numpy as jnp

def _softmax(x, axis=-1):
    return jax.nn.softmax(x, axis=axis)

def _gelu(x):
    return jax.nn.gelu(x, approximate=True)

def _silu(x):
    return jax.nn.silu(x)

def _sigmoid(x):
    return jax.nn.sigmoid(x)

def _layernorm(x, axis=-1, eps=1e-05):
    m = jnp.mean(x, axis=axis, keepdims=True)
    v = jnp.var(x, axis=axis, keepdims=True)
    return (x - m) / jnp.sqrt(v + eps)

def _scatter_add(tgt, idx, src, axis=0):
    return tgt.at[idx].add(src)

def _segment_sum(src, seg, n):
    return jax.ops.segment_sum(src, seg, n)
kernel_name = 'mk_gnn_resnorm_d4_gnn_r16_5ad15f'

def setup_inputs(seed: int=0):
    np.random.seed(seed)
    _w = jnp.asarray

    def _rec_inputs():
        import jax
        import jax.numpy as jnp
        _gk = jax.random.key(seed)
        x = -0.000202 + 1 * jax.random.normal(jax.random.fold_in(_gk, 1), (3125, 128), jnp.float32)
        _s = jax.random.randint(jax.random.fold_in(_gk, 2), (50000,), 0, 3125, jnp.int32)
        _d = jax.random.randint(jax.random.fold_in(_gk, 3), (50000,), 0, 3125, jnp.int32)
        _loop = jnp.arange(3125, dtype=jnp.int32)
        src = jnp.concatenate([_s, _d, _loop])
        dst = jnp.concatenate([_d, _s, _loop])
        _o = jnp.argsort(dst, stable=True)
        src = src[_o]
        dst = dst[_o]
        edge_weight = jax.random.uniform(jax.random.fold_in(_gk, 12), (103125,), jnp.float32, 0.0, 0.999999)
        return (x, src, dst, edge_weight)
    x, src, dst, edge_weight = _rec_inputs()

    def _L0_gnn_setup():
        import jax, jax.numpy as jnp
        import numpy as np
        import math
        N = 3125
        E = 50000
        HID = 128
        HEADS = 8
        DK = HID // HEADS
        EPS_LN = 1e-05

        def _layer_norm(x, g, b):
            mu = jnp.mean(x, axis=-1, keepdims=True)
            var = jnp.mean(jnp.square(x - mu), axis=-1, keepdims=True)
            return (x - mu) * jax.lax.rsqrt(var + EPS_LN) * g + b
        key = jax.random.key(seed)
        ks = jax.random.split(key, 20)
        s = 1.0 / math.sqrt(HID)
        inp = {'x': jax.random.normal(ks[0], (N, HID), jnp.float32), 'Wq': jax.random.normal(ks[1], (HID, HID), jnp.float32) * s, 'bq': jnp.zeros((HID,), jnp.float32), 'Wk': jax.random.normal(ks[2], (HID, HID), jnp.float32) * s, 'bk': jnp.zeros((HID,), jnp.float32), 'Wv': jax.random.normal(ks[3], (HID, HID), jnp.float32) * s, 'bv': jnp.zeros((HID,), jnp.float32), 'Wo': jax.random.normal(ks[4], (HID, HID), jnp.float32) * s, 'bo': jnp.zeros((HID,), jnp.float32), 'ln1_g': jnp.ones((HID,), jnp.float32), 'ln1_b': jnp.zeros((HID,), jnp.float32), 'W1': jax.random.normal(ks[5], (HID, 4 * HID), jnp.float32) * s, 'b1': jnp.zeros((4 * HID,), jnp.float32), 'W2': jax.random.normal(ks[6], (4 * HID, HID), jnp.float32) * (0.5 * s), 'b2': jnp.zeros((HID,), jnp.float32), 'ln2_g': jnp.ones((HID,), jnp.float32), 'ln2_b': jnp.zeros((HID,), jnp.float32), 'edge_index': jax.random.randint(ks[7], (2, E), 0, N, jnp.int64 if jax.config.jax_enable_x64 else jnp.int32)}
        return inp
    _L0_gnn_all = _L0_gnn_setup()
    _L0_gnn_in = {k: v for k, v in _L0_gnn_all.items() if k in ('Wq', 'bq', 'Wk', 'bk', 'Wv', 'bv', 'Wo', 'bo', 'ln1_g', 'ln1_b', 'W1', 'b1', 'W2', 'b2', 'ln2_g', 'ln2_b')}
    del _L0_gnn_all

    def _L1_gnn_setup():
        import jax, jax.numpy as jnp
        import numpy as np
        N_NODES = 3125
        N_EDGES = 100000
        D = 128
        N_LAYERS = 2
        NEG_SLOPE = 0.2

        def _gcn_layer(x, src, dst, ew, Ws, bs, Wn, bn, bias):
            n = x.shape[0]
            msg = x[src] * ew[:, None]
            agg = jax.ops.segment_sum(msg, dst, num_segments=n)
            agg = agg + x
            cnt = jax.ops.segment_sum(jnp.ones_like(ew), dst, num_segments=n) + 1.0
            neigh = agg / cnt[:, None]
            out = x @ Ws.T + bs + neigh @ Wn.T + bn + bias
            return jnp.where(out > 0, out, NEG_SLOPE * out)
        key = jax.random.key(seed)
        ks = jax.random.split(key, 10)
        user_embeddings = jax.random.normal(ks[0], (N_NODES, D), dtype=jnp.float32)
        social_edge_index = jax.random.randint(ks[1], (2, N_EDGES), 0, N_NODES, dtype=jnp.int64)
        social_edge_weights = jax.random.uniform(ks[2], (N_EDGES,), dtype=jnp.float32)
        s = 1.0 / np.sqrt(D)
        W_self = jax.random.uniform(ks[3], (N_LAYERS, D, D), minval=-s, maxval=s, dtype=jnp.float32)
        b_self = jax.random.uniform(ks[4], (N_LAYERS, D), minval=-s, maxval=s, dtype=jnp.float32)
        W_neigh = jax.random.uniform(ks[5], (N_LAYERS, D, D), minval=-s, maxval=s, dtype=jnp.float32)
        b_neigh = jax.random.uniform(ks[6], (N_LAYERS, D), minval=-s, maxval=s, dtype=jnp.float32)
        layer_bias = jnp.zeros((N_LAYERS, D), dtype=jnp.float32)
        W_agg = jax.random.uniform(ks[7], (D, D), minval=-s, maxval=s, dtype=jnp.float32)
        b_agg = jax.random.uniform(ks[8], (D,), minval=-s, maxval=s, dtype=jnp.float32)
        return {'user_embeddings': user_embeddings, 'social_edge_index': social_edge_index, 'social_edge_weights': social_edge_weights, 'W_self': W_self, 'b_self': b_self, 'W_neigh': W_neigh, 'b_neigh': b_neigh, 'layer_bias': layer_bias, 'W_agg': W_agg, 'b_agg': b_agg}
    _L1_gnn_all = _L1_gnn_setup()
    _L1_gnn_in = {k: v for k, v in _L1_gnn_all.items() if k in ('W_self', 'b_self', 'W_neigh', 'b_neigh', 'layer_bias', 'W_agg', 'b_agg')}
    del _L1_gnn_all

    def _L2_gnn_setup():
        import jax, jax.numpy as jnp
        import numpy as np
        N = 3125
        E = 50000
        F = 128
        HID = 128
        LN_EPS = 1e-05
        NEG_SLOPE = 0.2

        def _gatv2(x, Wl, bl, Wr, br, att, bias, src, dst, heads, outc, concat):
            n = x.shape[0]
            xl = (x @ Wl + bl).reshape(n, heads, outc)
            e_feat = jax.nn.leaky_relu(xl[src] + (x @ Wr + br).reshape(n, heads, outc)[dst], NEG_SLOPE)
            logits = jnp.einsum('ehc,hc->eh', e_feat, att)
            m = jax.ops.segment_max(logits, dst, num_segments=n)
            a = jnp.exp(logits - m[dst])
            denom = jax.ops.segment_sum(a, dst, num_segments=n)
            a = a / denom[dst]
            out = jax.ops.segment_sum(xl[src] * a[:, :, None], dst, num_segments=n)
            out = out.reshape(n, heads * outc) if concat else out.mean(axis=1)
            return out + bias

        def _ln(h, g, b):
            mu = h.mean(-1, keepdims=True)
            var = ((h - mu) ** 2).mean(-1, keepdims=True)
            return (h - mu) * jax.lax.rsqrt(var + LN_EPS) * g + b
        key = jax.random.key(seed)
        ks = jax.random.split(key, 32)
        g = lambda k, shape, s=0.05: jax.random.normal(k, shape, dtype=jnp.float32) * s
        inp = {}
        inp['x'] = jax.random.normal(ks[0], (N, F), dtype=jnp.float32)
        inp['edge_index'] = jax.random.randint(ks[1], (2, E), 0, N)
        i = 2
        inp['W1l'] = g(ks[i], (F, HID))
        inp['b1l'] = jnp.zeros((HID,), jnp.float32)
        inp['W1r'] = g(ks[i + 1], (F, HID))
        inp['b1r'] = jnp.zeros((HID,), jnp.float32)
        inp['a1'] = g(ks[i + 2], (4, HID // 4))
        inp['c1'] = jnp.zeros((HID,), jnp.float32)
        inp['g1'] = jnp.ones((HID,), jnp.float32)
        inp['be1'] = jnp.zeros((HID,), jnp.float32)
        inp['W2l'] = g(ks[i + 3], (HID, HID))
        inp['b2l'] = jnp.zeros((HID,), jnp.float32)
        inp['W2r'] = g(ks[i + 4], (HID, HID))
        inp['b2r'] = jnp.zeros((HID,), jnp.float32)
        inp['a2'] = g(ks[i + 5], (4, HID // 4))
        inp['c2'] = jnp.zeros((HID,), jnp.float32)
        inp['g2'] = jnp.ones((HID,), jnp.float32)
        inp['be2'] = jnp.zeros((HID,), jnp.float32)
        inp['W3l'] = g(ks[i + 6], (HID, HID))
        inp['b3l'] = jnp.zeros((HID,), jnp.float32)
        inp['W3r'] = g(ks[i + 7], (HID, HID))
        inp['b3r'] = jnp.zeros((HID,), jnp.float32)
        inp['a3'] = g(ks[i + 8], (1, HID))
        inp['c3'] = jnp.zeros((HID,), jnp.float32)
        inp['g3'] = jnp.ones((HID,), jnp.float32)
        inp['be3'] = jnp.zeros((HID,), jnp.float32)
        return inp
    _L2_gnn_all = _L2_gnn_setup()
    _L2_gnn_in = {k: v for k, v in _L2_gnn_all.items() if k in ('W1l', 'b1l', 'W1r', 'b1r', 'a1', 'c1', 'g1', 'be1', 'W2l', 'b2l', 'W2r', 'b2r', 'a2', 'c2', 'g2', 'be2', 'W3l', 'b3l', 'W3r', 'b3r', 'a3', 'c3', 'g3', 'be3')}
    del _L2_gnn_all

    def _L3_gnn_setup():
        import jax, jax.numpy as jnp
        import numpy as np
        EPS = 1e-05
        key = jax.random.key(seed)
        ks = jax.random.split(key, 4)
        N, E, D_IN, D_OUT = (625, 40000, 128, 128)
        x = jax.random.normal(ks[0], (N, D_IN), dtype=jnp.float32)
        edge_index = jax.random.randint(ks[1], (2, E), 0, N, dtype=jnp.int64)
        edge_weight = jax.random.uniform(ks[2], (E,), dtype=jnp.float32)
        W = jax.random.normal(ks[3], (D_IN, D_OUT), dtype=jnp.float32) / np.sqrt(D_IN)
        b = jnp.zeros((D_OUT,), dtype=jnp.float32)
        gamma = jnp.ones((D_OUT,), dtype=jnp.float32)
        beta = jnp.zeros((D_OUT,), dtype=jnp.float32)
        return {'x': x, 'edge_index': edge_index, 'edge_weight': edge_weight, 'W': W, 'b': b, 'gamma': gamma, 'beta': beta}
    _L3_gnn_all = _L3_gnn_setup()
    _L3_gnn_in = {k: v for k, v in _L3_gnn_all.items() if k in ('W', 'b', 'gamma', 'beta')}
    del _L3_gnn_all
    return {'x': x, 'src': src, 'dst': dst, 'edge_weight': edge_weight, 'L0_gnn_Wq': _L0_gnn_in['Wq'], 'L0_gnn_bq': _L0_gnn_in['bq'], 'L0_gnn_Wk': _L0_gnn_in['Wk'], 'L0_gnn_bk': _L0_gnn_in['bk'], 'L0_gnn_Wv': _L0_gnn_in['Wv'], 'L0_gnn_bv': _L0_gnn_in['bv'], 'L0_gnn_Wo': _L0_gnn_in['Wo'], 'L0_gnn_bo': _L0_gnn_in['bo'], 'L0_gnn_ln1_g': _L0_gnn_in['ln1_g'], 'L0_gnn_ln1_b': _L0_gnn_in['ln1_b'], 'L0_gnn_W1': _L0_gnn_in['W1'], 'L0_gnn_b1': _L0_gnn_in['b1'], 'L0_gnn_W2': _L0_gnn_in['W2'], 'L0_gnn_b2': _L0_gnn_in['b2'], 'L0_gnn_ln2_g': _L0_gnn_in['ln2_g'], 'L0_gnn_ln2_b': _L0_gnn_in['ln2_b'], 'L1_gnn_W_self': _L1_gnn_in['W_self'], 'L1_gnn_b_self': _L1_gnn_in['b_self'], 'L1_gnn_W_neigh': _L1_gnn_in['W_neigh'], 'L1_gnn_b_neigh': _L1_gnn_in['b_neigh'], 'L1_gnn_layer_bias': _L1_gnn_in['layer_bias'], 'L1_gnn_W_agg': _L1_gnn_in['W_agg'], 'L1_gnn_b_agg': _L1_gnn_in['b_agg'], 'L2_gnn_W1l': _L2_gnn_in['W1l'], 'L2_gnn_b1l': _L2_gnn_in['b1l'], 'L2_gnn_W1r': _L2_gnn_in['W1r'], 'L2_gnn_b1r': _L2_gnn_in['b1r'], 'L2_gnn_a1': _L2_gnn_in['a1'], 'L2_gnn_c1': _L2_gnn_in['c1'], 'L2_gnn_g1': _L2_gnn_in['g1'], 'L2_gnn_be1': _L2_gnn_in['be1'], 'L2_gnn_W2l': _L2_gnn_in['W2l'], 'L2_gnn_b2l': _L2_gnn_in['b2l'], 'L2_gnn_W2r': _L2_gnn_in['W2r'], 'L2_gnn_b2r': _L2_gnn_in['b2r'], 'L2_gnn_a2': _L2_gnn_in['a2'], 'L2_gnn_c2': _L2_gnn_in['c2'], 'L2_gnn_g2': _L2_gnn_in['g2'], 'L2_gnn_be2': _L2_gnn_in['be2'], 'L2_gnn_W3l': _L2_gnn_in['W3l'], 'L2_gnn_b3l': _L2_gnn_in['b3l'], 'L2_gnn_W3r': _L2_gnn_in['W3r'], 'L2_gnn_b3r': _L2_gnn_in['b3r'], 'L2_gnn_a3': _L2_gnn_in['a3'], 'L2_gnn_c3': _L2_gnn_in['c3'], 'L2_gnn_g3': _L2_gnn_in['g3'], 'L2_gnn_be3': _L2_gnn_in['be3'], 'L3_gnn_W': _L3_gnn_in['W'], 'L3_gnn_b': _L3_gnn_in['b'], 'L3_gnn_gamma': _L3_gnn_in['gamma'], 'L3_gnn_beta': _L3_gnn_in['beta']}

def reference(x, src, dst, edge_weight, L0_gnn_Wq, L0_gnn_bq, L0_gnn_Wk, L0_gnn_bk, L0_gnn_Wv, L0_gnn_bv, L0_gnn_Wo, L0_gnn_bo, L0_gnn_ln1_g, L0_gnn_ln1_b, L0_gnn_W1, L0_gnn_b1, L0_gnn_W2, L0_gnn_b2, L0_gnn_ln2_g, L0_gnn_ln2_b, L1_gnn_W_self, L1_gnn_b_self, L1_gnn_W_neigh, L1_gnn_b_neigh, L1_gnn_layer_bias, L1_gnn_W_agg, L1_gnn_b_agg, L2_gnn_W1l, L2_gnn_b1l, L2_gnn_W1r, L2_gnn_b1r, L2_gnn_a1, L2_gnn_c1, L2_gnn_g1, L2_gnn_be1, L2_gnn_W2l, L2_gnn_b2l, L2_gnn_W2r, L2_gnn_b2r, L2_gnn_a2, L2_gnn_c2, L2_gnn_g2, L2_gnn_be2, L2_gnn_W3l, L2_gnn_b3l, L2_gnn_W3r, L2_gnn_b3r, L2_gnn_a3, L2_gnn_c3, L2_gnn_g3, L2_gnn_be3, L3_gnn_W, L3_gnn_b, L3_gnn_gamma, L3_gnn_beta):
    import jax
    import jax.numpy as jnp

    def _L0_gnn_ref(x, Wq, bq, Wk, bk, Wv, bv, Wo, bo, ln1_g, ln1_b, W1, b1, W2, b2, ln2_g, ln2_b, edge_index):
        import jax, jax.numpy as jnp
        import numpy as np
        import math
        N = 3125
        E = 50000
        HID = 128
        HEADS = 8
        DK = HID // HEADS
        EPS_LN = 1e-05

        def _layer_norm(x, g, b):
            mu = jnp.mean(x, axis=-1, keepdims=True)
            var = jnp.mean(jnp.square(x - mu), axis=-1, keepdims=True)
            return (x - mu) * jax.lax.rsqrt(var + EPS_LN) * g + b
        n = x.shape[0]
        src, tgt = (edge_index[0], edge_index[1])
        Q = (x @ Wq + bq).reshape(n, HEADS, DK)
        K = (x @ Wk + bk).reshape(n, HEADS, DK)
        V = (x @ Wv + bv).reshape(n, HEADS, DK)
        scores = jnp.sum(Q[tgt] * K[src], axis=-1) / math.sqrt(DK)
        smax = jax.ops.segment_max(scores, tgt, num_segments=n)
        sexp = jnp.exp(scores - smax[tgt])
        ssum = jax.ops.segment_sum(sexp, tgt, num_segments=n)
        alpha = sexp / (ssum[tgt] + 1e-16)
        messages = alpha[:, :, None] * V[src]
        agg = jax.ops.segment_sum(messages, tgt, num_segments=n).reshape(n, HID)
        out = agg @ Wo + bo
        h = _layer_norm(x + out, ln1_g, ln1_b)
        ff = jax.nn.relu(h @ W1 + b1) @ W2 + b2
        return _layer_norm(h + ff, ln2_g, ln2_b)

    def _L1_gnn_ref(user_embeddings, social_edge_index, social_edge_weights, W_self, b_self, W_neigh, b_neigh, layer_bias, W_agg, b_agg):
        import jax, jax.numpy as jnp
        import numpy as np
        N_NODES = 3125
        N_EDGES = 100000
        D = 128
        N_LAYERS = 2
        NEG_SLOPE = 0.2

        def _gcn_layer(x, src, dst, ew, Ws, bs, Wn, bn, bias):
            n = x.shape[0]
            msg = x[src] * ew[:, None]
            agg = jax.ops.segment_sum(msg, dst, num_segments=n)
            agg = agg + x
            cnt = jax.ops.segment_sum(jnp.ones_like(ew), dst, num_segments=n) + 1.0
            neigh = agg / cnt[:, None]
            out = x @ Ws.T + bs + neigh @ Wn.T + bn + bias
            return jnp.where(out > 0, out, NEG_SLOPE * out)
        src = social_edge_index[0]
        dst = social_edge_index[1]
        x = user_embeddings
        for l in range(N_LAYERS):
            x = _gcn_layer(x, src, dst, social_edge_weights, W_self[l], b_self[l], W_neigh[l], b_neigh[l], layer_bias[l])
        return x @ W_agg.T + b_agg

    def _L2_gnn_ref(x, edge_index, W1l, b1l, W1r, b1r, a1, c1, g1, be1, W2l, b2l, W2r, b2r, a2, c2, g2, be2, W3l, b3l, W3r, b3r, a3, c3, g3, be3):
        import jax, jax.numpy as jnp
        import numpy as np
        N = 3125
        E = 50000
        F = 128
        HID = 128
        LN_EPS = 1e-05
        NEG_SLOPE = 0.2

        def _gatv2(x, Wl, bl, Wr, br, att, bias, src, dst, heads, outc, concat):
            n = x.shape[0]
            xl = (x @ Wl + bl).reshape(n, heads, outc)
            e_feat = jax.nn.leaky_relu(xl[src] + (x @ Wr + br).reshape(n, heads, outc)[dst], NEG_SLOPE)
            logits = jnp.einsum('ehc,hc->eh', e_feat, att)
            m = jax.ops.segment_max(logits, dst, num_segments=n)
            a = jnp.exp(logits - m[dst])
            denom = jax.ops.segment_sum(a, dst, num_segments=n)
            a = a / denom[dst]
            out = jax.ops.segment_sum(xl[src] * a[:, :, None], dst, num_segments=n)
            out = out.reshape(n, heads * outc) if concat else out.mean(axis=1)
            return out + bias

        def _ln(h, g, b):
            mu = h.mean(-1, keepdims=True)
            var = ((h - mu) ** 2).mean(-1, keepdims=True)
            return (h - mu) * jax.lax.rsqrt(var + LN_EPS) * g + b
        n = x.shape[0]
        loops = jnp.arange(n, dtype=edge_index.dtype)
        src = jnp.concatenate([edge_index[0], loops])
        dst = jnp.concatenate([edge_index[1], loops])
        h = _gatv2(x, W1l, b1l, W1r, b1r, a1, c1, src, dst, 4, HID // 4, True)
        h = jax.nn.relu(_ln(h, g1, be1))
        h = _gatv2(h, W2l, b2l, W2r, b2r, a2, c2, src, dst, 4, HID // 4, True)
        h = jax.nn.relu(_ln(h, g2, be2))
        h = _gatv2(h, W3l, b3l, W3r, b3r, a3, c3, src, dst, 1, HID, False)
        h = jax.nn.relu(_ln(h, g3, be3))
        return h

    def _L3_gnn_ref(x, edge_index, edge_weight, W, b, gamma, beta):
        import jax, jax.numpy as jnp
        import numpy as np
        EPS = 1e-05
        N = x.shape[0]
        src, dst = (edge_index[0], edge_index[1])
        deg = jax.ops.segment_sum(jnp.ones(dst.shape[0], dtype=x.dtype), dst, num_segments=N)
        deg_inv = (deg + 1.0) ** (-0.5)
        msgs = x[src] * deg_inv[src][:, None] * edge_weight[:, None]
        agg = jax.ops.segment_sum(msgs, dst, num_segments=N)
        agg = agg * deg_inv[:, None] + x
        h = jax.nn.gelu(agg @ W + b, approximate=False)
        mu = jnp.mean(h, axis=-1, keepdims=True)
        var = jnp.mean((h - mu) ** 2, axis=-1, keepdims=True)
        return (h - mu) * jax.lax.rsqrt(var + EPS) * gamma + beta
    edge_index = jnp.stack([src, dst])
    x = _layernorm(x + _L0_gnn_ref(x, L0_gnn_Wq, L0_gnn_bq, L0_gnn_Wk, L0_gnn_bk, L0_gnn_Wv, L0_gnn_bv, L0_gnn_Wo, L0_gnn_bo, L0_gnn_ln1_g, L0_gnn_ln1_b, L0_gnn_W1, L0_gnn_b1, L0_gnn_W2, L0_gnn_b2, L0_gnn_ln2_g, L0_gnn_ln2_b, edge_index), axis=-1)
    x = _layernorm(x + _L1_gnn_ref(x, edge_index, edge_weight, L1_gnn_W_self, L1_gnn_b_self, L1_gnn_W_neigh, L1_gnn_b_neigh, L1_gnn_layer_bias, L1_gnn_W_agg, L1_gnn_b_agg), axis=-1)
    x = _layernorm(x + _L2_gnn_ref(x, edge_index, L2_gnn_W1l, L2_gnn_b1l, L2_gnn_W1r, L2_gnn_b1r, L2_gnn_a1, L2_gnn_c1, L2_gnn_g1, L2_gnn_be1, L2_gnn_W2l, L2_gnn_b2l, L2_gnn_W2r, L2_gnn_b2r, L2_gnn_a2, L2_gnn_c2, L2_gnn_g2, L2_gnn_be2, L2_gnn_W3l, L2_gnn_b3l, L2_gnn_W3r, L2_gnn_b3r, L2_gnn_a3, L2_gnn_c3, L2_gnn_g3, L2_gnn_be3), axis=-1)
    x = _layernorm(x + _L3_gnn_ref(x, edge_index, edge_weight, L3_gnn_W, L3_gnn_b, L3_gnn_gamma, L3_gnn_beta), axis=-1)
    return x

_drawn_inputs = setup_inputs


def setup_inputs(seed=0):
    import zlib

    import numpy as np

    out = dict(_drawn_inputs(seed))
    spreads = {'L0_gnn_bq': (0.0, 0.751),
     'L0_gnn_bk': (0.0, 2.0),
     'L0_gnn_bv': (0.0, 0.1),
     'L0_gnn_bo': (0.0, 0.1),
     'L0_gnn_ln1_g': (1.0, 0.2),
     'L0_gnn_ln1_b': (0.0, 0.1),
     'L0_gnn_b1': (0.0, 0.1),
     'L0_gnn_b2': (0.0, 0.1),
     'L0_gnn_ln2_g': (1.0, 0.2),
     'L0_gnn_ln2_b': (0.0, 0.1),
     'L1_gnn_layer_bias': (0.0, 0.1),
     'L2_gnn_b1l': (0.0, 0.1),
     'L2_gnn_b1r': (0.0, 2.0),
     'L2_gnn_c1': (0.0, 0.1),
     'L2_gnn_g1': (1.0, 0.2),
     'L2_gnn_be1': (0.0, 0.1),
     'L2_gnn_b2l': (0.0, 0.1),
     'L2_gnn_b2r': (0.0, 2.0),
     'L2_gnn_c2': (0.0, 0.1),
     'L2_gnn_g2': (1.0, 0.2),
     'L2_gnn_be2': (0.0, 0.1),
     'L2_gnn_b3l': (0.0, 0.1),
     'L2_gnn_b3r': (0.0, 2.0),
     'L2_gnn_c3': (0.0, 0.1),
     'L2_gnn_g3': (1.0, 0.2),
     'L2_gnn_be3': (0.0, 0.1),
     'L3_gnn_b': (0.0, 0.1),
     'L3_gnn_gamma': (1.0, 0.2),
     'L3_gnn_beta': (0.0, 0.1)}
    factors = {'L2_gnn_W1r': 64.0,
     'L2_gnn_W2r': 64.0,
     'L2_gnn_a2': 46.265,
     'L2_gnn_W3r': 64.0,
     'L2_gnn_a3': 64.0}
    for name, (base, spread) in spreads.items():
        noise = np.random.default_rng([zlib.crc32(name.encode()), seed]).standard_normal(out[name].shape)
        drawn = base * np.exp(spread * noise) if base else spread * noise
        out[name] = jnp.asarray(drawn.astype(out[name].dtype))
    for name, factor in factors.items():
        out[name] = (out[name] * factor).astype(out[name].dtype)
    return out
```

```python
from contextlib import ExitStack

import concourse.bass as bass
import concourse.mybir as mybir

F32 = mybir.dt.float32
I32 = mybir.dt.int32
ALU = mybir.AluOpType
ACT = mybir.ActivationFunctionType
X_AXIS = mybir.AxisListType.X

P = 128
N_NODES = 3125
N_EDGES = 103125
D = 128
BLOCKS = -(-N_NODES // P)
GROUP = 4
WIDE = GROUP * D
GROUPS = -(-BLOCKS // GROUP)
BLOCKS_PAD = GROUPS * GROUP
NODES_PAD = BLOCKS_PAD * P
FULL_BLOCKS = N_NODES // P
LAST_NODES = N_NODES - FULL_BLOCKS * P

CHUNKS = -(-N_EDGES // P)
BODY = 16
TURNS = -(-(CHUNKS + BLOCKS - 1) // BODY)
STEPS = TURNS * BODY
STEP_GROUPS = STEPS // GROUP
BODY_GROUPS = BODY // GROUP
HALF = BODY // 2
STEP_COLS = -(-STEPS // P)
STEPS_PAD = STEP_COLS * P
EDGES_PER_ROW = CHUNKS + 2
TABLE_CHUNKS = EDGES_PER_ROW
FULL_ROWS = N_EDGES // EDGES_PER_ROW
LAST_EDGES = N_EDGES - FULL_ROWS * EDGES_PER_ROW
NO_NODE = 2 * 4096

EXTRA = 9
EXTRA_WIDE = 96
EXTRA_AT = 7 * 512
BIG = 1e30
SLOPE = 0.2
LN_EPS = 1e-5


class Count:

    def __init__(self, sem):
        self.sem, self.base = sem, 0

    def at(self, n):
        return n + self.base

    def advance(self, n):
        self.base += n


class Builder:
    def __init__(self, nc, ctx, ins, out):
        self.nc, self.ctx, self.ins, self.out = nc, ctx, ins, out
        self.counts = {}
        self.names = 0
        self.unrolled = set()
        self.pe_regs = None

    def sb(self, ctx, name, shape, dt=F32):
        self.names += 1
        return ctx.enter_context(self.nc.sbuf_tensor(f"{name}_{self.names}", shape, dt))

    def dram(self, name, shape, dt=F32):
        return self.nc.dram_tensor(f"scratch_{name}", shape, dt).ap()

    def count(self, name):
        if name not in self.counts:
            self.counts[name] = Count(self.ctx.enter_context(self.nc.semaphore(f"s_{name}")))
        return self.counts[name]

    def bank(self, b):
        return self.ps[:, b * 512:(b + 1) * 512]


class Chain:

    def __init__(self, eng, count):
        self.eng, self.count, self.n = eng, count, 0

    def __call__(self, ins):
        self.n += 1
        ins.then_inc(self.count.sem, 1)
        self.eng.wait_ge(self.count.sem, self.count.at(self.n))


def rows_of(vec, n):
    return bass.AP(tensor=vec.tensor, offset=vec.offset, ap=[[0, P], [1, n]])


def node_rows(table, lo, width):
    return table.rearrange("(b p) w -> p b w", p=P)[:, :, lo:lo + width]


def over_groups(t):
    return t.rearrange("p (k d) -> p k d", d=D)



def node_sweeps(B, steps):
    place, made = {}, {"tensor": 0, "vector": 0, "scalar": 0}
    for name, eng, after, emit in steps:
        place[name] = (eng, made[eng])
        made[eng] += 1
    sems = {e: B.count("sweep_" + e) for e in made}

    def program(which):
        def run(eng):
            for name, e, after, emit in steps:
                if e != which:
                    continue

                def one(g):
                    for a in after:
                        producer, sweep = place[a]
                        eng.wait_ge(sems[producer].sem, sems[producer].at(sweep * GROUPS + 1) + g)
                    emit(eng, g).then_inc(sems[which].sem, 1)
                if which == "tensor" or name in B.unrolled:
                    for g in range(GROUPS):
                        one(g)
                else:
                    with eng.Fori(0, GROUPS) as g:
                        one(g)
        return run

    with B.nc.Block() as block:
        block.tensor(program("tensor"))
        block.vector(program("vector"))
        block.scalar(program("scalar"))
    for e in made:
        sems[e].advance(made[e] * GROUPS)


def grp(t, g, width=WIDE):
    return t[:, bass.ds(g * width, width)]


def transpose_steps(B, name, src, dst, after):
    def turn(eng, g):
        for k in range(GROUP):
            c = g * WIDE + k * D
            ins = eng.transpose(B.ps[:, c:c + D], src[:, c:c + D], B.ident[:, :])
        return ins

    def keep(eng, g):
        return eng.activation(grp(dst, g), grp(B.ps, g), ACT.Copy)
    return [(name + ".turn", "tensor", after, turn), (name, "scalar", [name + ".turn"], keep)]


def matmul_step(name, B, parts, after):
    def mm(eng, g):
        for k in range(GROUP):
            c = g * WIDE + k * D
            for j, (xt, w) in enumerate(parts):
                ins = eng.matmul(B.ps[:, c:c + D], xt[:, c:c + D], w,
                                 start=(j == 0), stop=(j == len(parts) - 1))
        return ins
    return (name, "tensor", after, mm)


def add_row_step(name, dst, src, row, op, after):
    def f(eng, g):
        r = row[:, :].rearrange("p (o d) -> p o d", o=1).to_broadcast([P, GROUP, D])
        return eng.tensor_tensor(over_groups(grp(dst, g)), over_groups(grp(src, g)), r, op)
    return (name, "vector", after, f)


def add_step(name, dst, a, b, after, op=ALU.add):
    return (name, "vector", after, lambda eng, g: eng.tensor_tensor(grp(dst, g), grp(a, g), grp(b, g), op))


def scale_heads_step(name, dst, src, factor, heads, after):
    n = GROUP * heads

    def f(eng, g):
        s = grp(factor, g, n).rearrange("p (m o) -> p m o", o=1).to_broadcast([P, n, D // heads])
        return eng.tensor_tensor(grp(dst, g).rearrange("p (m d) -> p m d", m=n),
                                 grp(src, g).rearrange("p (m d) -> p m d", m=n), s, ALU.mult)
    return (name, "vector", after, f)


def leaky_step(name, dst, src, after):
    return (name, "vector", after, lambda eng, g: eng.scalar_tensor_tensor(
        out=grp(dst, g), in0=grp(src, g), scalar=SLOPE, in1=grp(src, g), op0=ALU.mult, op1=ALU.max))


def layernorm_steps(B, name, dst, src, after, gamma=None, beta=None):
    st, mv, rs = B.ln_stats, B.ln_mean_var, B.ln_rstd

    def stats(eng, g):
        for k in range(GROUP):
            ins = eng.bn_stats(st[:, bass.ds((g * GROUP + k) * 6, 6)], src[:, bass.ds(g * WIDE + k * D, D)])
        return ins

    def aggregate(eng, g):
        for k in range(GROUP):
            ins = eng.bn_aggr(mv[:, bass.ds((g * GROUP + k) * 2, 2)], st[:, bass.ds((g * GROUP + k) * 6, 6)])
        return ins

    def root(eng, g):
        var = grp(mv, g, GROUP * 2).rearrange("p (k c) -> p k c", c=2)[:, :, 1]
        return eng.activation(grp(rs, g, GROUP), var, ACT.Sqrt, bias=B.eps[:, 0:1])

    def inverse(eng, g):
        return eng.reciprocal(grp(rs, g, GROUP), grp(rs, g, GROUP))

    def normalise(eng, g):
        for k in range(GROUP):
            c = bass.ds(g * WIDE + k * D, D)
            ins = eng.tensor_scalar(dst[:, c], src[:, c], mv[:, bass.ds((g * GROUP + k) * 2, 1)],
                                    rs[:, bass.ds(g * GROUP + k, 1)], ALU.subtract, ALU.mult)
        return ins
    last = name if gamma is None else name + ".norm"
    B.unrolled.add(name + ".aggr")
    steps = [(name + ".stats", "vector", after, stats),
             (name + ".aggr", "vector", [name + ".stats"], aggregate),
             (name + ".root", "scalar", [name + ".aggr"], root),
             (name + ".inv", "vector", [name + ".root"], inverse),
             (last, "vector", [name + ".inv"] + list(after), normalise)]
    if gamma is not None:
        steps += [add_row_step(name + ".gamma", dst, dst, gamma, ALU.mult, [last]),
                  add_row_step(name, dst, dst, beta, ALU.add, [name + ".gamma"])]
    return steps


def load(B, pairs):
    landed = B.count("load")
    with B.nc.Block() as block:
        @block.sync
        def _(eng):
            for dst, src in pairs:
                eng.dma_start(dst, src, allow_slow_non_contiguous=True).then_inc(landed.sem, 16)
            eng.wait_ge(landed.sem, landed.at(16 * len(pairs)))
    landed.advance(16 * len(pairs))


def store(B, pairs):
    load(B, pairs)


def turn_weights(B, pairs):
    pe, act = B.count("turn_pe"), B.count("turn_act")
    with B.nc.Block() as block:
        @block.tensor
        def _(eng):
            for j, (_, src) in enumerate(pairs):
                eng.transpose(B.ps[:, j * 512:j * 512 + D], src, B.ident[:, :]).then_inc(pe.sem, 1)

        @block.scalar
        def _(eng):
            for j, (dst, _) in enumerate(pairs):
                eng.wait_ge(pe.sem, pe.at(j + 1))
                eng.activation(dst, B.ps[:, j * 512:j * 512 + D], ACT.Copy).then_inc(act.sem, 1)
    pe.advance(len(pairs))
    act.advance(len(pairs))



def backwards(row):
    return row[:, ::-1]


def lay_out_edges(B):
    nc = B.nc
    ins = B.ins
    tab = {k: B.dram("tab_" + k, [TABLE_CHUNKS, P], dt)
           for k, dt in (("src", I32), ("dst", I32), ("w", F32))}
    block_of_step = B.dram("block_of_step", [STEPS_PAD], F32)
    L = STEPS * P
    B.keys = B.dram("keys", [L + 2, 1])
    keys = B.keys.tensor
    flat = {"src": ins["src"], "dst": ins["dst"], "w": ins["edge_weight"]}

    with ExitStack() as ctx:
        full = {k: B.sb(ctx, "full_" + k, [P, EDGES_PER_ROW], F32 if k == "w" else I32) for k in tab}
        dst_f = B.sb(ctx, "dst_f", [P, EDGES_PER_ROW])
        junk = B.sb(ctx, "junk", [P, EDGES_PER_ROW])
        edge_of_block = B.sb(ctx, "edge_of_block", [P, BLOCKS - 1])
        below = B.sb(ctx, "below", [P, BLOCKS - 1])
        start_i = B.sb(ctx, "start_i", [P, BLOCKS - 1], I32)
        first_step = B.sb(ctx, "first_step", [P, BLOCKS - 1])
        iota_i = B.sb(ctx, "iota_i", [P, P], I32)
        step_i = B.sb(ctx, "step_i", [P, STEP_COLS], I32)
        block_i = B.sb(ctx, "block_i", [P, BLOCKS - 1], I32)
        step_f = B.sb(ctx, "step_f", [P, STEP_COLS])
        entered = B.sb(ctx, "entered", [P, STEP_COLS, BLOCKS - 1])
        block_f = B.sb(ctx, "block_f", [P, STEP_COLS])
        base_f = B.sb(ctx, "base_f", [P, STEP_COLS])
        chunk_f = B.sb(ctx, "chunk_f", [P, STEP_COLS])
        chunk_i = B.sb(ctx, "chunk_i", [P, STEP_COLS], I32)
        rows = {k: B.sb(ctx, "rows_" + k, [P, STEP_COLS, P], F32 if k == "w" else I32) for k in tab}
        src_f = B.sb(ctx, "src_f", [P, STEP_COLS, P])
        local = B.sb(ctx, "local", [P, STEP_COLS, P])
        key = B.sb(ctx, "key", [P, STEP_COLS, P])
        key_next = B.sb(ctx, "key_next", [P, STEP_COLS, P])
        halo = B.sb(ctx, "halo", [1, 2])
        reg_f = B.sb(ctx, "reg_f", [1, STEPS_PAD])
        ones = B.sb(ctx, "ones", [P, P])

        ve, po, pe, dma = (B.count(n) for n in ("edge_ve", "edge_po", "edge_pe", "edge_dma"))
        gat = B.count("edge_gather")
        act = B.count("edge_act")
        kept = [B.count(f"kept{q}") for q in range(BODY_GROUPS)]

        with nc.Block() as block:
            @block.vector
            def _(eng):
                eng.memset(full["src"][:, :], 0)
                eng.memset(full["dst"][:, :], NO_NODE)
                eng.memset(full["w"][:, :], 0.0)
                eng.memset(ones[:, :], 1.0)
                eng.memset(B.x[:, :], 0.0)
                eng.memset(B.eps[:, :], LN_EPS)
                eng.memset(B.zeros[:, :], 0.0)
                eng.memset(halo[:, 0:1], BIG)
                eng.memset(halo[:, 1:2], -2.0 * NO_NODE * BIG)
                eng.memset(B.ident[:, :], 0.0).then_inc(ve.sem, 1)

            @block.gpsimd
            def _(eng):
                eng.iota(iota_i[:, :], [[1, P]], base=0, channel_multiplier=0)
                eng.iota(step_i[:, :], [[P, STEP_COLS]], base=0, channel_multiplier=1)
                eng.iota(block_i[:, :], [[1, BLOCKS - 1]], base=1, channel_multiplier=0)
                eng.wait_ge(ve.sem, ve.at(1))
                eng.affine_select(out=B.ident[:, :], in_=B.ident[:, :], compare_op=ALU.not_equal, fill=1.0,
                                  base=0, pattern=[[-1, P]], channel_multiplier=1)
        ve.advance(1)

        with nc.Block() as block:
            @block.sync
            def _(eng):
                n = 0
                for k, t in full.items():
                    v = flat[k]
                    eng.dma_start(t[0:FULL_ROWS, :], v[0:FULL_ROWS * EDGES_PER_ROW].rearrange(
                        "(p j) -> p j", j=EDGES_PER_ROW)).then_inc(dma.sem, 16)
                    eng.dma_start(t[FULL_ROWS:FULL_ROWS + 1, 0:LAST_EDGES],
                                  v[FULL_ROWS * EDGES_PER_ROW:N_EDGES].rearrange(
                                      "(p j) -> p j", p=1)).then_inc(dma.sem, 16)
                    n += 2
                eng.dma_start(over_groups(B.x[:, 0:FULL_BLOCKS * D]),
                              ins["x"][0:FULL_BLOCKS * P, :].rearrange("(b p) d -> p b d", p=P)
                              ).then_inc(dma.sem, 16)
                eng.dma_start(B.x[0:LAST_NODES, FULL_BLOCKS * D:(FULL_BLOCKS + 1) * D],
                              ins["x"][FULL_BLOCKS * P:N_NODES, :]).then_inc(dma.sem, 16)
                n += 2
                eng.wait_ge(dma.sem, dma.at(16 * n))
                for q, (k, t) in enumerate(full.items()):
                    whole = bass.AP(tensor=tab[k].tensor, offset=0, ap=[[EDGES_PER_ROW, P], [1, EDGES_PER_ROW]])
                    eng.dma_start(whole, t[:, :]).then_inc(kept[q].sem, 16)
                eng.dma_start(bass.AP(tensor=keys, offset=0, ap=[[1, 1], [1, 1]]), halo[:, 0:1]).then_inc(kept[3].sem, 16)
                eng.dma_start(bass.AP(tensor=keys, offset=L + 1, ap=[[1, 1], [1, 1]]), halo[:, 1:2]).then_inc(dma.sem, 16)
                n += 1
                eng.wait_ge(dma.sem, dma.at(16 * n))
                for c in kept:
                    eng.wait_ge(c.sem, c.at(16))
        dma.advance(16 * (3 * 2 + 2 + 1))
        for c in kept:
            c.advance(16)

        with nc.Block() as block:
            @block.vector
            def _(eng):
                link = Chain(eng, ve)
                link(eng.tensor_copy(dst_f[:, :], full["dst"][:, :]))
                eng.tensor_copy(B.iota[:, :], iota_i[:, :])
                eng.tensor_copy(step_f[:, :], step_i[:, :])
                link(eng.tensor_copy(edge_of_block[:, :], block_i[:, :]))
                link(eng.tensor_scalar(first_step[:, :], edge_of_block[:, :], float(P), None, ALU.mult))
                with eng.Fori(0, BLOCKS - 1) as b:
                    eng.wait_ge(ve.sem, ve.at(3) + b)
                    eng.tensor_scalar(junk[:, :], dst_f[:, :], first_step[:, bass.ds(b, 1)], 0.0, ALU.is_lt,
                                      ALU.add, accum_out=below[:, bass.ds(b, 1)]).then_inc(ve.sem, 1)
                eng.wait_ge(pe.sem, pe.at(1))
                link.n += BLOCKS - 1
                link(eng.tensor_copy(start_i[:, :], B.ps[:, 0:BLOCKS - 1]))
                link(eng.tensor_scalar(start_i[:, :], start_i[:, :], 7, None, ALU.arith_shift_right))
                link(eng.tensor_copy(first_step[:, :], start_i[:, :]))
                link(eng.tensor_tensor(first_step[:, :], first_step[:, :], edge_of_block[:, :], ALU.add))
                link(eng.tensor_tensor(
                    entered[:, :, :],
                    first_step[:, :].rearrange("p (o b) -> p o b", o=1).to_broadcast([P, STEP_COLS, BLOCKS - 1]),
                    step_f[:, :].rearrange("p (s o) -> p s o", o=1).to_broadcast([P, STEP_COLS, BLOCKS - 1]),
                    ALU.is_le))
                link(eng.tensor_reduce(block_f[:, :], entered[:, :, :], X_AXIS, ALU.add))
                link(eng.tensor_tensor(chunk_f[:, :], step_f[:, :], block_f[:, :], ALU.subtract))
                link(eng.tensor_scalar(chunk_f[:, :], chunk_f[:, :], float(TABLE_CHUNKS - 1), None, ALU.min))
                link(eng.tensor_copy(chunk_i[:, :], chunk_f[:, :]))
                link(eng.tensor_scalar(base_f[:, :], block_f[:, :], float(P), None, ALU.mult))

            @block.tensor
            def _(eng):
                eng.wait_ge(ve.sem, ve.at(3 + BLOCKS - 1))
                eng.matmul(B.ps[:, 0:BLOCKS - 1], ones[:, :], below[:, :], start=True, stop=True).then_inc(pe.sem, 1)
        ve.advance(3 + BLOCKS - 1 + 10)
        pe.advance(1)

        with nc.Block() as block:
            @block.gpsimd
            def _(eng):
                n = 0
                for k in tab:
                    for c in range(STEP_COLS):
                        eng.indirect_dma_start(rows[k][:, c, :], None, tab[k][:, :],
                                               bass.IndirectOffsetOnAxis(ap=chunk_i[:, c:c + 1], axis=0)
                                               ).then_inc(gat.sem, 16)
                        n += 1
                eng.dma_start(block_of_step.rearrange("(c p) -> p c", p=P), block_f[:, :],
                              allow_slow_non_contiguous=True).then_inc(gat.sem, 16)
                n += 1
                eng.wait_ge(gat.sem, gat.at(16 * n))
        gat.advance(16 * (3 * STEP_COLS + 1))

        with nc.Block() as block:
            @block.sync
            def _(eng):
                eng.dma_start(reg_f[:, :], block_of_step.rearrange("(o s) -> o s", o=1)).then_inc(dma.sem, 16)
                eng.wait_ge(ve.sem, ve.at(4))
                full_cols = STEPS // P
                for c in range(STEP_COLS):
                    m = min(P, STEPS - c * P)
                    eng.dma_start(bass.AP(tensor=keys, offset=1 + c * P * P, ap=[[P, m], [1, P]]),
                                  key[0:m, c, :]).then_inc(dma.sem, 16)
                eng.wait_ge(dma.sem, dma.at(16 * (1 + STEP_COLS)))
                for c in range(STEP_COLS):
                    m = min(P, STEPS - c * P)
                    eng.dma_start(key_next[0:m, c, :],
                                  bass.AP(tensor=keys, offset=2 + c * P * P, ap=[[P, m], [1, P]])).then_inc(dma.sem, 16)

            @block.vector
            def _(eng):
                link = Chain(eng, ve)
                eng.tensor_copy(src_f[:, :, :], rows["src"][:, :, :])
                eng.memset(key_next[:, :, :], 0.0)
                base = base_f[:, :].rearrange("p (c o) -> p c o", o=1).to_broadcast([P, STEP_COLS, P])
                link(eng.tensor_tensor(local[:, :, :], rows["dst"][:, :, :], base, ALU.subtract))
                link(eng.tensor_scalar(local[:, :, :], local[:, :, :], -0.5, P - 0.5, ALU.max, ALU.min))
                link(eng.tensor_tensor(key[:, :, :], local[:, :, :], base, ALU.add))
                link(eng.tensor_scalar(key[:, :, :], key[:, :, :], -BIG, None, ALU.mult))
                eng.wait_ge(dma.sem, dma.at(16 * (1 + 2 * STEP_COLS)))
                link(eng.tensor_tensor(key_next[:, :, :], key[:, :, :], key_next[:, :, :], ALU.not_equal))
                link(eng.tensor_scalar(B.sum_col[:, :], reg_f[:, :], float(D), None, ALU.mult))
                link(eng.tensor_scalar(B.extra_col[:, :], reg_f[:, :], float(EXTRA), float(EXTRA_AT), ALU.mult, ALU.add))

            @block.tensor
            def _(eng):
                eng.wait_ge(ve.sem, ve.at(2))
                for j, t in enumerate((src_f, local, rows["w"])):
                    if j == 2:
                        eng.wait_ge(act.sem, act.at(1))
                    for c in range(STEP_COLS):
                        at = (j % 2) * 1024 + c * P
                        ins = eng.transpose(B.ps[:, at:at + P], t[:, c, :], B.ident[:, :])
                    ins.then_inc(pe.sem, 1)
                eng.wait_ge(act.sem, act.at(2))
                eng.wait_ge(ve.sem, ve.at(5))
                for c in range(STEP_COLS):
                    ins = eng.transpose(B.ps[:, 1024 + c * P:1024 + (c + 1) * P], key_next[:, c, :], B.ident[:, :])
                ins.then_inc(pe.sem, 1)

            @block.scalar
            def _(eng):
                for j, t in enumerate((B.edge_src, B.edge_local, B.edge_weight, B.edge_last)):
                    eng.wait_ge(pe.sem, pe.at(j + 1))
                    at = (j % 2) * 1024
                    eng.activation(t[:, :], B.ps[:, at:at + STEPS_PAD], ACT.Copy).then_inc(act.sem, 1)
        ve.advance(7)
        dma.advance(16 * (1 + 2 * STEP_COLS))
        pe.advance(4)
        act.advance(4)



def one_hot(B, eng, dst, step):
    loc = B.edge_local[:, bass.ds(step, GROUP)].rearrange("p (k o) -> p k o", o=1).to_broadcast([P, GROUP, P])
    io = B.iota[:, :].rearrange("p (o n) -> p o n", o=1).to_broadcast([P, GROUP, P])
    return eng.tensor_tensor(dst, io, loc, ALU.is_equal)


def block_registers(B, eng, table, step, bank):
    regs = B.pe_regs[bank * HALF:(bank + 1) * HALF]
    eng.load(regs, table[0:1, bass.ds(step, HALF)])
    return [eng.snap(r, min_val=0, max_val=(BLOCKS - 1) * D if bank == 0 else EXTRA_AT + (BLOCKS - 1) * EXTRA) for r in regs]


def gather_rows(B, eng, slots, table, width, turn, s, sems):
    eng.indirect_dma_start(slots[:, s * width:(s + 1) * width], None, table,
                           bass.IndirectOffsetOnAxis(ap=B.index_ring[:, s:s + 1], axis=0)
                           ).then_inc(sems[s].sem, 16)


def clear_sums(B, eng):
    for b in range(8):
        eng.matmul(B.bank(b), B.zeros[:, 0:P], B.zeros[:, :], start=True, stop=True, skip_group_check=True)


def gcn_pass(B, table):
    nc = B.nc
    with ExitStack() as ctx:
        rows = B.sb(ctx, "gcn_rows", [P, BODY * D])
        hot = B.sb(ctx, "gcn_hot", [P, BODY, P])
        landed = [B.count(f"gather{s}") for s in range(BODY)]
        index, hot_made, used = (B.count(n) for n in ("index", "hot", "used"))
        wait_holder = B.count("wait_holder")
        with nc.Block() as block:
            @block.scalar
            def _(eng):
                with eng.Fori(0, TURNS) as i:
                    for h in range(2):
                        eng.wait_ge(used.sem, used.at(h + 1) + i * 2)
                        eng.activation(B.index_ring[:, h * HALF:(h + 1) * HALF],
                                       B.edge_src[:, bass.ds(i * BODY + h * HALF, HALF)], ACT.Copy
                                       ).then_inc(index.sem, 1)

            @block.gpsimd
            def _(eng):
                with eng.Fori(0, TURNS) as i:
                    for h in range(2):
                        eng.wait_ge(index.sem, index.at(h + 1) + i * 2)
                        eng.sem_inc(wait_holder.sem, 1)
                        for s in range(h * HALF, (h + 1) * HALF):
                            gather_rows(B, eng, rows, table, D, i, s, landed)

            @block.vector
            def _(eng):
                with eng.Fori(0, TURNS) as i:
                    for h in range(2):
                        eng.wait_ge(used.sem, used.at(h + 1) + i * 2)
                        for s in range(h * HALF, (h + 1) * HALF):
                            t = i * BODY + s
                            ins = eng.tensor_scalar(hot[:, s, :], B.iota[:, :], B.edge_local[:, bass.ds(t, 1)],
                                                    B.edge_weight[:, bass.ds(t, 1)], ALU.is_equal, ALU.mult)
                        ins.then_inc(hot_made.sem, 1)

            @block.tensor
            def _(eng):
                eng.sem_inc(used.sem, 2)
                clear_sums(B, eng)
                with eng.Fori(0, TURNS) as i:
                    for h in range(2):
                        cols = block_registers(B, eng, B.sum_col, i * BODY + h * HALF, 0)
                        eng.wait_ge(hot_made.sem, hot_made.at(h + 1) + i * 2)
                        for k in range(HALF):
                            s = h * HALF + k
                            eng.wait_ge(landed[s].sem, landed[s].at(16) + i * 16)
                            ins = eng.matmul(B.ps[:, bass.ds(cols[k], D)], hot[:, s, :],
                                             rows[:, s * D:(s + 1) * D], start=False, stop=True,
                                             skip_group_check=True)
                        ins.then_inc(used.sem, 1)
        for c in landed:
            c.advance(16 * TURNS)
        index.advance(2 * TURNS)
        hot_made.advance(2 * TURNS)
        used.advance(2 * TURNS + 2)


def score_pass(B, table, width, heads, queries, att, logits):
    nc = B.nc
    dim = D // heads
    with ExitStack() as ctx:
        rows = B.sb(ctx, "rows", [P, BODY * width])
        hot = B.sb(ctx, "hot", [P, 2, GROUP, P])
        hot_t = B.sb(ctx, "hot_t", [P, 2, GROUP * P])
        z = B.sb(ctx, "z", [P, 2, WIDE])
        landed = [B.count(f"gather{s}") for s in range(BODY)]
        kept = [B.count(f"kept{q}") for q in range(BODY_GROUPS)]
        index, hot_made, turned, hot_kept, asked, zed = (
            B.count(n) for n in ("index", "hot", "turned", "hot_kept", "asked", "zed"))
        wait_holder = B.count("wait_holder")
        per = 2 if att is None else 4

        def group_rows(q, lo):
            return rows[:, q * GROUP * width:(q + 1) * GROUP * width].rearrange(
                "p (k w) -> p k w", w=width)[:, :, lo:lo + D]

        with nc.Block() as block:
            @block.gpsimd
            def _(eng):
                with eng.Fori(0, TURNS) as i:
                    for h in range(2):
                        eng.wait_ge(index.sem, index.at(h + 1) + i * 2)
                        for q in range(2 * h, 2 * h + 2):
                            eng.wait_ge(kept[q].sem, kept[q].at(0) + i * 16)
                            eng.sem_inc(wait_holder.sem, 1)
                            for s in range(q * GROUP, (q + 1) * GROUP):
                                gather_rows(B, eng, rows, table, width, i, s, landed)

            @block.sync
            def _(eng):
                with eng.Fori(0, TURNS) as i:
                    for q in range(BODY_GROUPS):
                        for s in range(q * GROUP, (q + 1) * GROUP):
                            eng.wait_ge(landed[s].sem, landed[s].at(16) + i * 16)
                        eng.dma_start(over_groups(B.spool[bass.ds((i * BODY_GROUPS + q) * P, P), :]),
                                      group_rows(q, width - D)).then_inc(kept[q].sem, 16)
                for q in range(BODY_GROUPS):
                    eng.wait_ge(kept[q].sem, kept[q].at(16 * TURNS))

            @block.scalar
            def _(eng):
                with eng.Fori(0, TURNS) as i:
                    for q in range(BODY_GROUPS):
                        if q % 2 == 0:
                            h = q // 2
                            eng.wait_ge(zed.sem, zed.at((2 * h + 2) * per) + i * (BODY_GROUPS * per))
                            eng.activation(B.index_ring[:, h * HALF:(h + 1) * HALF],
                                           B.edge_src[:, bass.ds(i * BODY + h * HALF, HALF)], ACT.Copy
                                           ).then_inc(index.sem, 1)
                        n = i * BODY_GROUPS + q
                        eng.wait_ge(turned.sem, turned.at(3) + n)
                        eng.wait_ge(asked.sem, asked.at(1) + n)
                        eng.activation(hot_t[:, q % 2, :], B.bank(q % 2), ACT.Copy).then_inc(hot_kept.sem, 1)

            @block.vector
            def _(eng):
                eng.sem_inc(zed.sem, BODY_GROUPS * per)

                def make_hot(n, slot):
                    eng.wait_ge(turned.sem, turned.at(1) + n)
                    one_hot(B, eng, hot[:, slot, :, :], n * GROUP).then_inc(hot_made.sem, 1)

                make_hot(0, 0)
                with eng.Fori(0, TURNS) as i:
                    for q in range(BODY_GROUPS):
                        n = i * BODY_GROUPS + q
                        make_hot(n + 1, (q + 1) % 2)
                        eng.wait_ge(asked.sem, asked.at(3) + n)
                        for s in range(q * GROUP, (q + 1) * GROUP):
                            eng.wait_ge(landed[s].sem, landed[s].at(16) + i * 16)
                        zz = z[:, q % 2, :]
                        query = B.bank(2 + q % 2)
                        done = zed.at(BODY_GROUPS * per) + n * per

                        def then(j, ins):
                            ins.then_inc(zed.sem, 1)
                            eng.wait_ge(zed.sem, done + (j + 1))
                        out = logits[:, bass.ds(n * (GROUP * heads), GROUP * heads)]
                        if att is None:
                            then(0, eng.tensor_tensor(over_groups(zz), over_groups(query), group_rows(q, 0), ALU.mult))
                        else:
                            then(0, eng.tensor_tensor(over_groups(zz), over_groups(query), group_rows(q, 0), ALU.add))
                            then(1, eng.scalar_tensor_tensor(out=zz, in0=zz, scalar=SLOPE, in1=zz,
                                                             op0=ALU.mult, op1=ALU.max))
                            a = att[:, :].rearrange("p (o d) -> p o d", o=1).to_broadcast([P, GROUP, D])
                            then(2, eng.tensor_tensor(over_groups(zz), over_groups(zz), a, ALU.mult))
                        eng.tensor_reduce(out, zz.rearrange("p (m d) -> p m d", d=dim), X_AXIS, ALU.add
                                          ).then_inc(zed.sem, 1)

            @block.tensor
            def _(eng):
                eng.sem_inc(turned.sem, 2)
                eng.sem_inc(asked.sem, 2)
                with eng.Fori(0, TURNS) as i:
                    for q in range(BODY_GROUPS):
                        n = i * BODY_GROUPS + q
                        if q % 2 == 0:
                            cols = block_registers(B, eng, B.sum_col, i * BODY + q * GROUP, 0)
                        eng.wait_ge(hot_made.sem, hot_made.at(1) + n)
                        for k in range(GROUP):
                            ins = eng.transpose(B.ps[:, (q % 2) * 512 + k * P:(q % 2) * 512 + (k + 1) * P],
                                                hot[:, q % 2, k, :], B.ident[:, :])
                        ins.then_inc(turned.sem, 1)
                        eng.wait_ge(hot_kept.sem, hot_kept.at(1) + n)
                        eng.wait_ge(zed.sem, zed.at((BODY_GROUPS - 1) * per) + n * per)
                        for k in range(GROUP):
                            at = (2 + q % 2) * 512 + k * D
                            ins = eng.matmul(B.ps[:, at:at + D], hot_t[:, q % 2, k * P:(k + 1) * P],
                                             queries[:, bass.ds(cols[(q % 2) * GROUP + k], D)],
                                             start=True, stop=True)
                        ins.then_inc(asked.sem, 1)
        for c in landed:
            c.advance(16 * TURNS)
        for c in kept:
            c.advance(16 * TURNS)
        index.advance(2 * TURNS)
        hot_made.advance(STEP_GROUPS + 1)
        turned.advance(STEP_GROUPS + 2)
        hot_kept.advance(STEP_GROUPS)
        asked.advance(STEP_GROUPS + 2)
        zed.advance((STEP_GROUPS + BODY_GROUPS) * per)


def segment_softmax(B, heads, scale, logits, extra, with_max):
    nc = B.nc
    slices = min(P // heads, 64)
    R = heads * slices
    per_slice = STEPS // slices
    L = per_slice * P
    batch = per_slice // 13
    n_batch = per_slice // batch
    BW = batch * P
    keys = B.keys.tensor
    with ExitStack() as ctx:
        lt = B.sb(ctx, "lt", [R, L])
        fw = B.sb(ctx, "fw", [R, L])
        key = B.sb(ctx, "keyrow", [R, L + 2])
        reset = B.sb(ctx, "reset", [R, L + 1], mybir.dt.bfloat16)
        ends = B.sb(ctx, "ends", [R, 4])
        row = B.sb(ctx, "row", [1, 4 * R + 1])
        open_f = B.sb(ctx, "open_f", [1, R + 1])
        open_b = B.sb(ctx, "open_b", [1, R + 1])
        pen = B.sb(ctx, "pen", [1, 2 * R])
        carry_row = B.sb(ctx, "carry_row", [1, 2 * R])
        carry = B.sb(ctx, "carry", [R, 2])
        stage = B.sb(ctx, "stage", [P, 2, batch * R])
        pe, act, ve, dma, staged = (B.count(n) for n in ("seg_pe", "seg_act", "seg_ve", "seg_dma", "seg_staged"))
        lg = logits[:, 0:STEPS * heads].rearrange("p (s t h) -> p t h s", s=slices, h=heads)
        ex = extra[:, :].rearrange("p (s t c) -> p t c s", s=slices, c=EXTRA)
        chain_n = 17
        ops = 2 if with_max else 1
        with nc.Block() as block:
            @block.sync
            def _(eng):
                for h in range(heads):
                    eng.dma_start(key[h * slices:(h + 1) * slices, :],
                                  bass.AP(tensor=keys, offset=0, ap=[[L, slices], [1, L + 2]])).then_inc(dma.sem, 16)

            @block.tensor
            def _(eng):
                for j in range(n_batch):
                    if j >= 7:
                        eng.wait_ge(act.sem, act.at(j - 6))
                    eng.wait_ge(staged.sem, staged.at(j + 1))
                    for m in range(batch):
                        at = (j % 7) * 512 + m * P
                        ins = eng.transpose(B.ps[0:R, at:at + P],
                                            stage[:, j % 2, m * R:(m + 1) * R], B.ident[:, :])
                    ins.then_inc(pe.sem, 1)
                eng.wait_ge(ve.sem, ve.at(4))
                eng.wait_ge(act.sem, act.at(n_batch))
                for c in range(4):
                    ins = eng.transpose(B.ps[0:1, c * 128:c * 128 + R], ends[:, c:c + 1], B.ident[0:R, 0:R])
                ins.then_inc(pe.sem, 1)
                eng.wait_ge(ve.sem, ve.at(12))
                for c in range(2):
                    ins = eng.transpose(B.ps[0:R, 512 + c:512 + c + 1], carry_row[:, c * R:(c + 1) * R],
                                        B.ident[0:1, 0:1])
                ins.then_inc(pe.sem, 1)
                eng.wait_ge(ve.sem, ve.at(chain_n))
                for j in range(n_batch):
                    if j >= 7:
                        eng.wait_ge(ve.sem, ve.at(chain_n + (j - 6) * ops))
                    for m in range(batch):
                        at = (j % 7) * 512 + m * P
                        g = j * batch + m
                        ins = eng.transpose(B.ps[:, at:at + R], lt[:, g * P:(g + 1) * P], B.ident[0:R, 0:R])
                    ins.then_inc(pe.sem, 1)

            @block.scalar
            def _(eng):
                for j in range(n_batch):
                    eng.wait_ge(pe.sem, pe.at(j + 1))
                    eng.activation(lt[:, j * BW:(j + 1) * BW], B.ps[0:R, (j % 7) * 512:(j % 7) * 512 + BW],
                                   ACT.Copy).then_inc(act.sem, 1)
                for j in range(n_batch):
                    t = slice(j * batch, (j + 1) * batch)
                    eng.wait_ge(ve.sem, ve.at(chain_n + (j + 1) * ops))
                    eng.activation(ex[:, t, 0:heads, :], lg[:, t, :, :], ACT.Exp, scale=scale
                                   ).then_inc(act.sem, 1)

            @block.vector
            def _(eng):
                link = Chain(eng, ve)
                eng.memset(open_f[:, 0:1], -BIG)
                eng.memset(open_b[:, R:R + 1], -BIG)
                eng.memset(row[:, 4 * R:4 * R + 1], -BIG)
                if not with_max:
                    eng.memset(extra[:, :].rearrange("p (t c) -> p t c", c=EXTRA)[:, :, heads:EXTRA], 1.0)
                for j in range(n_batch):
                    if j >= 2:
                        eng.wait_ge(pe.sem, pe.at(j - 1))
                    eng.tensor_copy(stage[:, j % 2, :].rearrange("p (t h s) -> p t h s", t=batch, h=heads),
                                    lg[:, j * batch:(j + 1) * batch, :, :]).then_inc(staged.sem, 1)
                eng.wait_ge(dma.sem, dma.at(16 * heads))
                link(eng.tensor_tensor(reset[:, :], key[:, 1:L + 2], key[:, 0:L + 1], ALU.subtract))
                eng.tensor_tensor(ends[:, 2:3], key[:, L:L + 1], key[:, 1:2], ALU.subtract)
                eng.tensor_copy(ends[:, 3:4], reset[:, 0:1])
                eng.wait_ge(act.sem, act.at(n_batch))
                link(eng.tensor_tensor_scan(fw[:, :], reset[:, 0:L], lt[:, :], -BIG, ALU.add, ALU.max))
                link(eng.tensor_tensor_scan(backwards(lt[:, :]), backwards(reset[:, 1:L + 1]), backwards(fw[:, :]),
                                            -BIG, ALU.add, ALU.max))
                eng.tensor_copy(ends[:, 0:1], fw[:, L - 1:L])
                link(eng.tensor_copy(ends[:, 1:2], lt[:, 0:1]))
                eng.wait_ge(pe.sem, pe.at(n_batch + 1))
                link(eng.tensor_copy(row[:, 0:4 * R].rearrange("p (c r) -> p c r", c=4),
                                     B.ps[0:1, 0:512].rearrange("p (c r) -> p c r", c=4)[:, :, 0:R]))
                fwd_end, bwd_end, through, going_on = (row[:, c * R:(c + 1) * R] for c in range(4))
                going_on_next = row[:, 3 * R + 1:4 * R + 1]
                link(eng.tensor_tensor(pen[:, 0:R], going_on, through, ALU.add))
                link(eng.tensor_tensor(pen[:, R:2 * R], going_on_next, through, ALU.add))
                link(eng.tensor_tensor_scan(open_f[:, 1:R + 1], pen[:, 0:R], fwd_end, -BIG, ALU.add, ALU.max))
                link(eng.tensor_tensor_scan(backwards(open_b[:, 0:R]), backwards(pen[:, R:2 * R]),
                                            backwards(bwd_end), -BIG, ALU.add, ALU.max))
                link(eng.tensor_tensor(carry_row[:, 0:R], open_f[:, 0:R], going_on, ALU.add))
                link(eng.tensor_tensor(carry_row[:, R:2 * R], open_b[:, 1:R + 1], going_on_next, ALU.add))
                link(eng.tensor_scalar(carry_row[:, :], carry_row[:, :], -BIG, None, ALU.max))
                eng.wait_ge(pe.sem, pe.at(n_batch + 2))
                link(eng.tensor_copy(carry[:, :], B.ps[0:R, 512:514]))
                link(eng.tensor_scalar(fw[:, :], key[:, 1:L + 1], key[:, 1:2], None, ALU.subtract))
                link(eng.scalar_tensor_tensor(out=lt[:, :], in0=fw[:, :], scalar=carry[:, 0:1], in1=lt[:, :],
                                              op0=ALU.add, op1=ALU.max))
                link(eng.tensor_scalar(fw[:, :], key[:, 1:L + 1], -1.0, key[:, L:L + 1], ALU.mult, ALU.add))
                link(eng.scalar_tensor_tensor(out=lt[:, :], in0=fw[:, :], scalar=carry[:, 1:2], in1=lt[:, :],
                                              op0=ALU.add, op1=ALU.max))
                assert link.n == chain_n
                last = B.edge_last[:, 0:STEPS].rearrange("p (s t o) -> p t o s", s=slices, o=1)
                for j in range(n_batch):
                    eng.wait_ge(pe.sem, pe.at(n_batch + 3 + j))
                    t = slice(j * batch, (j + 1) * batch)
                    top = B.ps[:, (j % 7) * 512:(j % 7) * 512 + 512].rearrange(
                        "p (t q) -> p t q", q=P)[:, 0:batch, 0:R].rearrange("p t (h s) -> p t h s", h=heads)
                    if with_max:
                        eng.tensor_tensor(ex[:, t, heads:2 * heads, :], top,
                                          last[:, t, :, :].to_broadcast([P, batch, heads, slices]),
                                          ALU.mult).then_inc(ve.sem, 1)
                    eng.tensor_tensor(lg[:, t, :, :], lg[:, t, :, :], top, ALU.subtract).then_inc(ve.sem, 1)
        pe.advance(2 * n_batch + 2)
        act.advance(2 * n_batch)
        ve.advance(chain_n + n_batch * ops)
        dma.advance(16 * heads)
        staged.advance(n_batch)


def value_pass(B, heads, extra, extra_width):
    nc = B.nc
    dim = D // heads
    with ExitStack() as ctx:
        vals = B.sb(ctx, "vals", [P, BODY_GROUPS, WIDE])
        hot = B.sb(ctx, "vhot", [P, BODY_GROUPS, GROUP, P])
        mix = B.sb(ctx, "mix", [P, BODY_GROUPS, WIDE])
        loaded = [B.count(f"loaded{q}") for q in range(BODY_GROUPS)]
        side = B.sb(ctx, "side", [P, BODY_GROUPS, GROUP * EXTRA_WIDE])
        mixed, used, sided = (B.count(n) for n in ("mixed", "used", "sided"))
        blank = B.count("blank")
        with nc.Block() as block:
            @block.sync
            def _(eng):
                with eng.Fori(0, TURNS) as i:
                    for q in range(BODY_GROUPS):
                        n = i * BODY_GROUPS + q
                        eng.wait_ge(mixed.sem, mixed.at(1) + n)
                        eng.dma_start(vals[:, q, :], B.spool[bass.ds(n * P, P), :]).then_inc(loaded[q].sem, 16)

            @block.scalar
            def _(eng):
                eng.wait_ge(blank.sem, blank.at(1))
                with eng.Fori(0, TURNS) as i:
                    for q in range(BODY_GROUPS):
                        n = i * BODY_GROUPS + q
                        eng.wait_ge(used.sem, used.at(1) + n)
                        eng.activation(side[:, q, :].rearrange("p (k c) -> p k c", c=EXTRA_WIDE)[:, :, 0:extra_width],
                                       extra[:, bass.ds(n * (GROUP * EXTRA), GROUP * EXTRA)].rearrange(
                                           "p (k c) -> p k c", c=EXTRA)[:, :, 0:extra_width],
                                       ACT.Copy).then_inc(sided.sem, 1)

            @block.vector
            def _(eng):
                eng.memset(side[:, :, :], 0.0).then_inc(blank.sem, 1)
                eng.sem_inc(mixed.sem, BODY_GROUPS)
                with eng.Fori(0, TURNS) as i:
                    for q in range(BODY_GROUPS):
                        n = i * BODY_GROUPS + q
                        eng.wait_ge(used.sem, used.at(1) + n)
                        one_hot(B, eng, hot[:, q, :, :], n * GROUP)
                        eng.wait_ge(loaded[q].sem, loaded[q].at(16) + i * 16)
                        f = extra[:, bass.ds(n * (GROUP * EXTRA), GROUP * EXTRA)].rearrange(
                            "p (k c) -> p k c", c=EXTRA)[:, :, 0:heads].rearrange(
                            "p k (h o) -> p k h o", o=1).to_broadcast([P, GROUP, heads, dim])
                        eng.tensor_tensor(mix[:, q, :].rearrange("p (k h d) -> p k h d", k=GROUP, h=heads),
                                          vals[:, q, :].rearrange("p (k h d) -> p k h d", k=GROUP, h=heads),
                                          f, ALU.mult).then_inc(mixed.sem, 1)

            @block.tensor
            def _(eng):
                eng.sem_inc(used.sem, BODY_GROUPS)
                clear_sums(B, eng)
                with eng.Fori(0, TURNS) as i:
                    for q in range(BODY_GROUPS):
                        n = i * BODY_GROUPS + q
                        if q % 2 == 0:
                            cols = block_registers(B, eng, B.sum_col, i * BODY + q * GROUP, 0)
                            ecols = block_registers(B, eng, B.extra_col, i * BODY + q * GROUP, 1)
                        eng.wait_ge(mixed.sem, mixed.at(BODY_GROUPS + 1) + n)
                        eng.wait_ge(sided.sem, sided.at(1) + n)
                        for k in range(GROUP):
                            r = (q % 2) * GROUP + k
                            eng.matmul(B.ps[:, bass.ds(cols[r], D)], hot[:, q, k, :],
                                       mix[:, q, k * D:(k + 1) * D], start=False, stop=True,
                                       skip_group_check=True)
                            ins = eng.matmul(B.ps[:, bass.ds(ecols[r], EXTRA_WIDE)], hot[:, q, k, :],
                                             side[:, q, k * EXTRA_WIDE:(k + 1) * EXTRA_WIDE],
                                             start=False, stop=True, skip_group_check=True)
                        ins.then_inc(used.sem, 1)
        for c in loaded:
            c.advance(16 * TURNS)
        sided.advance(STEP_GROUPS)
        blank.advance(1)
        mixed.advance(STEP_GROUPS + BODY_GROUPS)
        used.advance(STEP_GROUPS + BODY_GROUPS)


def vector_work(B, ops):
    done = B.count("small")

    def program(which):
        def run(eng):
            for n, (e, emit) in enumerate(ops):
                if e == which:
                    if n:
                        eng.wait_ge(done.sem, done.at(n))
                    emit(eng).then_inc(done.sem, 1)
        return run
    with B.nc.Block() as block:
        block.vector(program("vector"))
        block.scalar(program("scalar"))
    done.advance(len(ops))


def extras(B, lo, hi):
    return B.bank(7)[:, 0:BLOCKS_PAD * EXTRA].rearrange("p (b c) -> p b c", c=EXTRA)[:, :, lo:hi]



def attention_layer(B):
    w = {k: B.ins["L0_gnn_" + k] for k in ("Wq", "bq", "Wk", "bk", "Wv", "bv", "Wo", "bo", "ln1_g", "ln1_b",
                                          "W1", "b1", "W2", "b2", "ln2_g", "ln2_b")}
    heads, hidden = 8, 4
    table = B.dram("kv", [NODES_PAD, 2 * D])
    with ExitStack() as ctx:
        inv = B.sb(ctx, "inv", [P, BLOCKS_PAD * heads])
        with ExitStack() as ectx:
            extra = B.sb(ectx, "extra", [P, STEPS * EXTRA])
            with ExitStack() as lctx:
                logits = B.sb(lctx, "logits", [P, STEPS * heads])
                with ExitStack() as pctx:
                    q = B.sb(pctx, "q", [P, GROUPS * WIDE])
                    with ExitStack() as kctx:
                        k_, v_, xt = (B.sb(kctx, n, [P, GROUPS * WIDE]) for n in ("k", "v", "xt"))
                        wt = {n: B.sb(kctx, n, [P, D]) for n in ("Wq", "Wk", "Wv", "bq", "bk", "bv")}
                        load(B, [(wt[n][:, :], w[n]) for n in ("Wq", "Wk", "Wv")]
                             + [(wt[n][:, :], rows_of(w[n], D)) for n in ("bq", "bk", "bv")])
                        steps = transpose_steps(B, "xt", B.x, xt, [])
                        before = "xt"
                        for dst, c in ((q, "q"), (k_, "k"), (v_, "v")):
                            steps.append(matmul_step(c + "mm", B, [(xt, wt["W" + c][:, :])], [before]))
                            steps.append(add_row_step(c, dst, B.ps, wt["b" + c], ALU.add, [c + "mm"]))
                            before = c
                        node_sweeps(B, steps)
                        store(B, [(node_rows(table, 0, D), over_groups(k_[:, :])),
                                  (node_rows(table, D, D), over_groups(v_[:, :]))])
                    score_pass(B, table, 2 * D, heads, q, None, logits)
                segment_softmax(B, heads, 1.0 / (D // heads) ** 0.5, logits, extra, False)
            value_pass(B, heads, extra, heads + 1)
        vector_work(B, [
            ("vector", lambda e: e.tensor_copy(B.degree[:, :].rearrange("p (b o) -> p b o", o=1), extras(B, heads, heads + 1))),
            ("vector", lambda e: e.tensor_scalar(inv[:, :].rearrange("p (b h) -> p b h", h=heads), extras(B, 0, heads),
                                                 1e-16, None, ALU.add)),
            ("vector", lambda e: e.reciprocal(inv[:, :], inv[:, :])),
            ("vector", lambda e: e.tensor_scalar(B.degree_1[:, :], B.degree[:, :], 1.0, None, ALU.add)),
            ("vector", lambda e: e.reciprocal(B.inv_degree[:, :], B.degree_1[:, :])),
            ("scalar", lambda e: e.activation(B.root_degree[:, :], B.degree_1[:, :], ACT.Sqrt)),
            ("vector", lambda e: e.reciprocal(B.root_degree[:, :], B.root_degree[:, :])),
        ])
        agg, tr = (B.sb(ctx, n, [P, GROUPS * WIDE]) for n in ("agg", "tr"))
        h1 = [B.sb(ctx, f"h1_{c}", [P, GROUPS * WIDE]) for c in range(hidden)]
        wo = B.sb(ctx, "wo", [P, D])
        w1 = B.sb(ctx, "w1", [P, hidden * D])
        w2 = B.sb(ctx, "w2", [P, hidden, D])
        b1 = B.sb(ctx, "b1", [P, hidden])
        vec = {n: B.sb(ctx, n, [P, D]) for n in ("bo", "b2", "ln1_g", "ln1_b", "ln2_g", "ln2_b")}
        load(B, [(wo[:, :], w["Wo"]), (w1[:, :], w["W1"]), (w2[:, :, :], w["W2"].rearrange("(c p) d -> p c d", p=P)),
                 (b1[:, :], w["b1"].rearrange("(c p) -> p c", p=P))] + [(vec[n][:, :], rows_of(w[n], D)) for n in vec])

        def hidden_mm(c):
            return lambda eng, g: eng.matmul(B.bank(g), w1[:, c * D:(c + 1) * D],
                                             tr[:, g * WIDE:(g + 1) * WIDE], start=True, stop=True)

        def hidden_relu(c):
            return lambda eng, g: eng.activation(grp(h1[c], g), grp(B.ps, g), ACT.Relu, bias=b1[:, c:c + 1])
        steps = [scale_heads_step("agg", agg, B.ps, inv, heads, [])]
        steps += transpose_steps(B, "aggt", agg, tr, ["agg"])
        steps += [matmul_step("out", B, [(tr, wo[:, :])], ["aggt"]),
                  add_row_step("out_b", agg, B.ps, vec["bo"], ALU.add, ["out"]),
                  add_step("res1", agg, agg, B.x, ["out_b"])]
        steps += layernorm_steps(B, "ln1", agg, agg, ["res1"], vec["ln1_g"], vec["ln1_b"])
        steps += transpose_steps(B, "ht", agg, tr, ["ln1"])
        before = "ht"
        for c in range(hidden):
            steps += [(f"ff{c}", "tensor", [before], hidden_mm(c)),
                      (f"relu{c}", "scalar", [f"ff{c}"], hidden_relu(c))]
            before = f"relu{c}"
        steps += [matmul_step("ff", B, [(h1[c], w2[:, c, :]) for c in range(hidden)], [before]),
                  add_row_step("ff_b", tr, B.ps, vec["b2"], ALU.add, ["ff"]),
                  add_step("res2", agg, agg, tr, ["ff_b"])]
        steps += layernorm_steps(B, "ln2", agg, agg, ["res2"], vec["ln2_g"], vec["ln2_b"])
        steps += [add_step("res3", B.x, B.x, agg, ["ln2"])]
        steps += layernorm_steps(B, "x", B.x, B.x, ["res3"])
        node_sweeps(B, steps)


def gcn_layers(B):
    ins = B.ins
    layers = 2
    table = B.dram("gcn", [NODES_PAD, D])
    with ExitStack() as ctx:
        h, agg, tr, trx = (B.sb(ctx, n, [P, GROUPS * WIDE]) for n in ("h", "gagg", "gtr", "gtrx"))
        raw = {k: B.sb(ctx, k, [P, D]) for k in ("self0", "self1", "neigh0", "neigh1", "out")}
        wt = {k: B.sb(ctx, k + "_t", [P, D]) for k in raw}
        bias = {l: [B.sb(ctx, f"bias{l}{j}", [P, D]) for j in range(3)] for l in range(layers)}
        b_out = B.sb(ctx, "b_out", [P, D])
        load(B, [(raw["self0"][:, :], ins["L1_gnn_W_self"][0]), (raw["self1"][:, :], ins["L1_gnn_W_self"][1]),
                 (raw["neigh0"][:, :], ins["L1_gnn_W_neigh"][0]), (raw["neigh1"][:, :], ins["L1_gnn_W_neigh"][1]),
                 (raw["out"][:, :], ins["L1_gnn_W_agg"]), (b_out[:, :], rows_of(ins["L1_gnn_b_agg"], D))]
             + [(bias[l][j][:, :], rows_of(ins["L1_gnn_" + n][l], D))
                for l in range(layers) for j, n in enumerate(("b_self", "b_neigh", "layer_bias"))])
        turn_weights(B, [(wt[k][:, :], raw[k][:, :]) for k in raw])
        vector_work(B, [("vector", lambda e, l=l, j=j: e.tensor_tensor(bias[l][0][:, :], bias[l][0][:, :],
                                                                       bias[l][j][:, :], ALU.add))
                        for l in range(layers) for j in (1, 2)])
        cur = B.x
        for l in range(layers):
            store(B, [(node_rows(table, 0, D), over_groups(cur[:, :]))])
            gcn_pass(B, table)
            steps = [add_step("sum", agg, B.ps, cur, []),
                     scale_heads_step("mean", agg, agg, B.inv_degree, 1, ["sum"])]
            steps += transpose_steps(B, "aggt", agg, tr, ["mean"])
            steps += transpose_steps(B, "xt", cur, trx, ["aggt"])
            steps += [matmul_step("mm", B, [(trx, wt[f"self{l}"][:, :]), (tr, wt[f"neigh{l}"][:, :])], ["aggt", "xt"]),
                      add_row_step("pre", agg, B.ps, bias[l][0], ALU.add, ["mm"]),
                      leaky_step("h", h, agg, ["pre"])]
            if l == layers - 1:
                steps += transpose_steps(B, "ht", h, tr, ["h"])
                steps += [matmul_step("mm2", B, [(tr, wt["out"][:, :])], ["ht"]),
                          add_row_step("o", agg, B.ps, b_out, ALU.add, ["mm2"]),
                          add_step("res", B.x, B.x, agg, ["o"])]
                steps += layernorm_steps(B, "x", B.x, B.x, ["res"])
            node_sweeps(B, steps)
            cur = h


def gatv2_layers(B):
    table = B.dram("gat", [NODES_PAD, D])
    with ExitStack() as ctx:
        h, xl, xr = (B.sb(ctx, n, [P, GROUPS * WIDE]) for n in ("gh", "xl", "xr"))
        wt = {n: B.sb(ctx, "gat_" + n, [P, D]) for n in ("Wl", "Wr", "bl", "br", "a", "c", "g", "be")}
        for layer, heads in ((1, 4), (2, 4), (3, 1)):
            w = {n: B.ins[f"L2_gnn_{n[0]}{layer}{n[1:]}" if n[0] in "W" or n in ("bl", "br")
                          else f"L2_gnn_{n}{layer}"] for n in wt}
            load(B, [(wt[n][:, :], w[n]) for n in ("Wl", "Wr")]
                 + [(wt[n][:, :], rows_of(w[n], D)) for n in wt if n not in ("Wl", "Wr")])
            cur = B.x if layer == 1 else h
            with ExitStack() as lctx:
                own = B.sb(lctx, "own", [P, BLOCKS_PAD * heads])
                with ExitStack() as tctx:
                    tr, z = (B.sb(tctx, n, [P, GROUPS * WIDE]) for n in ("gat_tr", "gat_z"))
                    steps = transpose_steps(B, "xt", cur, tr, [])
                    steps += [matmul_step("lmm", B, [(tr, wt["Wl"][:, :])], ["xt"]),
                              add_row_step("l", xl, B.ps, wt["bl"], ALU.add, ["lmm"]),
                              matmul_step("rmm", B, [(tr, wt["Wr"][:, :])], ["l"]),
                              add_row_step("r", xr, B.ps, wt["br"], ALU.add, ["rmm"]),
                              add_step("z", z, xl, xr, ["r"]),
                              leaky_step("lz", z, z, ["z"]),
                              add_row_step("az", z, z, wt["a"], ALU.mult, ["lz"]),
                              ("own", "vector", ["az"], lambda eng, g: eng.tensor_reduce(
                                  grp(own, g, GROUP * heads), grp(z, g).rearrange("p (m d) -> p m d", d=D // heads),
                                  X_AXIS, ALU.add))]
                    node_sweeps(B, steps)
                    store(B, [(node_rows(table, 0, D), over_groups(xl[:, :]))])
                with ExitStack() as ectx:
                    extra = B.sb(ectx, "gextra", [P, STEPS * EXTRA])
                    with ExitStack() as sctx:
                        logits = B.sb(sctx, "glogits", [P, STEPS * heads])
                        score_pass(B, table, D, heads, xr, wt["a"], logits)
                        segment_softmax(B, heads, 1.0, logits, extra, True)
                    value_pass(B, heads, extra, 2 * heads)
                top, tot, new, we, ws = (B.sb(lctx, n, [P, BLOCKS_PAD * heads]) for n in ("top", "tot", "new", "we", "ws"))
                none = B.sb(lctx, "none", [P, BLOCKS_PAD])

                def by_node(t):
                    return t[:, :].rearrange("p (b h) -> p b h", h=heads)

                def vv(dst, a, b, op):
                    return ("vector", lambda e: e.tensor_tensor(dst, a, b, op))
                vector_work(B, [
                    ("vector", lambda e: e.tensor_scalar(none[:, :], B.degree[:, :], 0.5, -BIG, ALU.is_lt, ALU.mult)),
                    vv(by_node(top), extras(B, heads, 2 * heads), none[:, :].rearrange("p (b o) -> p b o", o=1)
                       .to_broadcast([P, BLOCKS_PAD, heads]), ALU.add),
                    vv(new[:, :], top[:, :], own[:, :], ALU.max),
                    vv(we[:, :], top[:, :], new[:, :], ALU.subtract),
                    vv(ws[:, :], own[:, :], new[:, :], ALU.subtract),
                    ("scalar", lambda e: e.activation(we[:, :], we[:, :], ACT.Exp)),
                    ("scalar", lambda e: e.activation(ws[:, :], ws[:, :], ACT.Exp)),
                    vv(by_node(tot), extras(B, 0, heads), by_node(we), ALU.mult),
                    vv(tot[:, :], tot[:, :], ws[:, :], ALU.add),
                    ("vector", lambda e: e.reciprocal(tot[:, :], tot[:, :])),
                    vv(we[:, :], we[:, :], tot[:, :], ALU.mult),
                    vv(ws[:, :], ws[:, :], tot[:, :], ALU.mult),
                ])
                steps = [scale_heads_step("e", h, B.ps, we, heads, []),
                         scale_heads_step("s", xl, xl, ws, heads, []),
                         add_step("sum", h, h, xl, ["e", "s"]),
                         add_row_step("c", h, h, wt["c"], ALU.add, ["sum"])]
                steps += layernorm_steps(B, "ln", h, h, ["c"], wt["g"], wt["be"])
                steps += [("h", "scalar", ["ln"], lambda eng, g: eng.activation(grp(h, g), grp(h, g), ACT.Relu))]
                if layer == 3:
                    steps += [add_step("res", B.x, B.x, h, ["h"])]
                    steps += layernorm_steps(B, "x", B.x, B.x, ["res"])
                node_sweeps(B, steps)


def normalised_gcn_layer(B):
    table = B.dram("norm", [NODES_PAD, D])
    ins = B.ins
    with ExitStack() as ctx:
        a, tr = (B.sb(ctx, n, [P, GROUPS * WIDE]) for n in ("na", "ntr"))
        wt = {n: B.sb(ctx, "n_" + n, [P, D]) for n in ("W", "b", "gamma", "beta")}
        load(B, [(wt["W"][:, :], ins["L3_gnn_W"])]
             + [(wt[n][:, :], rows_of(ins["L3_gnn_" + n], D)) for n in ("b", "gamma", "beta")])
        node_sweeps(B, [scale_heads_step("s", a, B.x, B.root_degree, 1, [])])
        store(B, [(node_rows(table, 0, D), over_groups(a[:, :]))])
        gcn_pass(B, table)
        steps = [scale_heads_step("s", a, B.ps, B.root_degree, 1, []),
                 add_step("sum", a, a, B.x, ["s"])]
        steps += transpose_steps(B, "t", a, tr, ["sum"])
        steps += [matmul_step("mm", B, [(tr, wt["W"][:, :])], ["t"]),
                  add_row_step("b", a, B.ps, wt["b"], ALU.add, ["mm"]),
                  ("gelu", "scalar", ["b"], lambda eng, g: eng.activation(grp(a, g), grp(a, g), ACT.Gelu))]
        steps += layernorm_steps(B, "ln", a, a, ["gelu"], wt["gamma"], wt["beta"])
        steps += [add_step("res", a, a, B.x, ["ln"])]
        steps += layernorm_steps(B, "x", B.x, a, ["res"])
        node_sweeps(B, steps)
    store(B, [(B.out[0:FULL_BLOCKS * P, :].rearrange("(b p) d -> p b d", p=P), over_groups(B.x[:, 0:FULL_BLOCKS * D])),
              (B.out[FULL_BLOCKS * P:N_NODES, :], B.x[0:LAST_NODES, FULL_BLOCKS * D:(FULL_BLOCKS + 1) * D])])


def build(nc, ins, out):
    with ExitStack() as ctx:
        B = Builder(nc, ctx, ins, out)
        B.ps = ctx.enter_context(nc.psum_tensor("sums", [P, 8 * 512], F32))
        B.x = B.sb(ctx, "x", [P, GROUPS * WIDE])
        B.ident = B.sb(ctx, "ident", [P, P])
        B.zeros = B.sb(ctx, "zeros", [P, 512], mybir.dt.bfloat16)
        B.iota = B.sb(ctx, "iota", [P, P])
        B.eps = B.sb(ctx, "eps", [P, 1])
        B.edge_src, B.edge_local, B.edge_weight, B.edge_last = (
            B.sb(ctx, n, [P, STEPS_PAD]) for n in ("edge_src", "edge_local", "edge_weight", "edge_last"))
        B.index_ring = B.sb(ctx, "index_ring", [P, BODY], I32)
        B.sum_col = B.sb(ctx, "sum_col", [1, STEPS_PAD], I32)
        B.extra_col = B.sb(ctx, "extra_col", [1, STEPS_PAD], I32)
        B.ln_stats = B.sb(ctx, "ln_stats", [P, BLOCKS_PAD * 6])
        B.ln_mean_var = B.sb(ctx, "ln_mean_var", [P, BLOCKS_PAD * 2])
        B.ln_rstd = B.sb(ctx, "ln_rstd", [P, BLOCKS_PAD])
        B.degree, B.degree_1, B.inv_degree, B.root_degree = (
            B.sb(ctx, n, [P, BLOCKS_PAD]) for n in ("degree", "degree_1", "inv_degree", "root_degree"))
        B.spool = B.dram("spool", [STEP_GROUPS * P, WIDE])
        B.pe_regs = [nc.tensor.alloc_register(f"block_reg{j}") for j in range(2 * HALF)]
        lay_out_edges(B)
        attention_layer(B)
        gcn_layers(B)
        gatv2_layers(B)
        normalised_gcn_layer(B)


def kernel(**inputs):
    import numpy as np
    import concourse.bacc as bacc
    from concourse.bass_utils import run_bass_kernel_spmd

    nc = bacc.Bacc("TRN2", target_bir_lowering=False, num_devices=1)
    arrays, handles = {}, {}
    for name, value in inputs.items():
        a = np.ascontiguousarray(value)
        arrays["in_" + name] = a
        handles[name] = nc.dram_tensor("in_" + name, a.shape, mybir.dt.from_np(a.dtype), kind="ExternalInput").ap()
    out = nc.dram_tensor("out", (N_NODES, D), F32, kind="ExternalOutput").ap()
    build(nc, handles, out)
    result = run_bass_kernel_spmd(nc, [arrays], core_ids=[0])
    return result.results[0]["out"]
```

```python
from contextlib import ExitStack

import concourse.bass as bass
import concourse.mybir as mybir

F32 = mybir.dt.float32
I32 = mybir.dt.int32
ALU = mybir.AluOpType
ACT = mybir.ActivationFunctionType
X_AXIS = mybir.AxisListType.X

P = 128
N_NODES = 3125
N_EDGES = 103125
D = 128
BLOCKS = -(-N_NODES // P)
GROUP = 4
WIDE = GROUP * D
GROUPS = -(-BLOCKS // GROUP)
BLOCKS_PAD = GROUPS * GROUP
NODES_PAD = BLOCKS_PAD * P
FULL_BLOCKS = N_NODES // P
LAST_NODES = N_NODES - FULL_BLOCKS * P

CHUNKS = -(-N_EDGES // P)
BODY = 16
TURNS = -(-(CHUNKS + BLOCKS - 1) // BODY)
STEPS = TURNS * BODY
STEP_GROUPS = STEPS // GROUP
BODY_GROUPS = BODY // GROUP
HALF = BODY // 2
STEP_COLS = -(-STEPS // P)
STEPS_PAD = STEP_COLS * P
EDGES_PER_ROW = CHUNKS + 2
TABLE_CHUNKS = EDGES_PER_ROW
FULL_ROWS = N_EDGES // EDGES_PER_ROW
LAST_EDGES = N_EDGES - FULL_ROWS * EDGES_PER_ROW
NO_NODE = 2 * 4096

EXTRA = 9
COLUMNS = 8 * 512
PARTS = 3
PART_COLS = PARTS * EXTRA
PART_WIDE = 128
EXTRA_SPLIT = 10
EXTRA_AT = BLOCKS * D
EXTRA_REST_AT = 7 * 512
assert EXTRA_AT + (EXTRA_SPLIT - 1) * PART_COLS + PART_WIDE <= EXTRA_REST_AT
assert EXTRA_REST_AT + (BLOCKS - EXTRA_SPLIT - 1) * PART_COLS + PART_WIDE <= COLUMNS
BIG = 1e30
SLOPE = 0.2
LN_EPS = 1e-5


class Count:

    def __init__(self, sem):
        self.sem, self.base = sem, 0

    def at(self, n):
        return n + self.base

    def advance(self, n):
        self.base += n


class Builder:
    def __init__(self, nc, ctx, ins, out):
        self.nc, self.ctx, self.ins, self.out = nc, ctx, ins, out
        self.counts = {}
        self.names = 0

    def sb(self, ctx, name, shape, dt=F32):
        self.names += 1
        return ctx.enter_context(self.nc.sbuf_tensor(f"{name}_{self.names}", shape, dt))

    def dram(self, name, shape, dt=F32):
        return self.nc.dram_tensor(f"scratch_{name}", shape, dt).ap()

    def fresh(self):
        self.names += 1
        return self.names

    def count(self, name):
        if name not in self.counts:
            self.counts[name] = Count(self.ctx.enter_context(self.nc.semaphore(f"s_{name}")))
        return self.counts[name]

    def bank(self, b):
        return self.ps[:, b * 512:(b + 1) * 512]


class Chain:

    def __init__(self, eng, count):
        self.eng, self.count, self.n = eng, count, 0

    def __call__(self, ins):
        self.n += 1
        ins.then_inc(self.count.sem, 1)
        self.eng.wait_ge(self.count.sem, self.count.at(self.n))


def rows_of(vec, n):
    return bass.AP(tensor=vec.tensor, offset=vec.offset, ap=[[0, P], [1, n]])


def node_rows(table, lo, width):
    return table.rearrange("(b p) w -> p b w", p=P)[:, :, lo:lo + width]


def over_groups(t):
    return t.rearrange("p (k d) -> p k d", d=D)



def node_sweeps(B, steps):
    place, made = {}, {"tensor": 0, "vector": 0, "scalar": 0, "sync": 0}
    for name, eng, after, emit in steps:
        place[name] = (eng, made[eng])
        made[eng] += 1
    sems = {e: B.count("sweep_" + e) for e in made}

    def program(which):
        def run(eng):
            for name, e, after, emit in steps:
                if e != which:
                    continue

                def one(g):
                    for a in after:
                        producer, sweep = place[a]
                        eng.wait_ge(sems[producer].sem, sems[producer].at(sweep * GROUPS + 1) + g)
                    emit(eng, g).then_inc(sems[which].sem, 16 if which == "sync" else 1)
                for g in range(GROUPS):
                    one(g)
            if which == "sync" and made["sync"]:
                eng.wait_ge(sems["sync"].sem, sems["sync"].at(16 * made["sync"] * GROUPS))
        return run

    with B.nc.Block() as block:
        block.tensor(program("tensor"))
        block.vector(program("vector"))
        block.scalar(program("scalar"))
        block.sync(program("sync"))
    for e in made:
        sems[e].advance(made[e] * GROUPS * (16 if e == "sync" else 1))


def grp(t, g, width=WIDE):
    return t[:, bass.ds(g * width, width)]


def store_step(name, table, lo, src, after):
    return (name, "sync", after, lambda eng, g: eng.dma_start(
        node_rows(table, lo, D)[:, g * GROUP:(g + 1) * GROUP, :], over_groups(grp(src, g))))


def transpose_steps(B, name, src, dst, after):
    def turn(eng, g):
        for k in range(GROUP):
            c = g * WIDE + k * D
            ins = eng.transpose(B.ps[:, c:c + D], src[:, c:c + D], B.ident[:, :])
        return ins

    def keep(eng, g):
        return eng.activation(grp(dst, g), grp(B.ps, g), ACT.Copy)
    return [(name + ".turn", "tensor", after, turn), (name, "scalar", [name + ".turn"], keep)]


def matmul_step(name, B, parts, after):
    def mm(eng, g):
        for k in range(GROUP):
            c = g * WIDE + k * D
            for j, (xt, w) in enumerate(parts):
                ins = eng.matmul(B.ps[:, c:c + D], xt[:, c:c + D], w,
                                 start=(j == 0), stop=(j == len(parts) - 1))
        return ins
    return (name, "tensor", after, mm)


def add_row_step(name, dst, src, row, op, after):
    def f(eng, g):
        r = row[:, :].rearrange("p (o d) -> p o d", o=1).to_broadcast([P, GROUP, D])
        return eng.tensor_tensor(over_groups(grp(dst, g)), over_groups(grp(src, g)), r, op)
    return (name, "vector", after, f)


def add_step(name, dst, a, b, after, op=ALU.add):
    return (name, "vector", after, lambda eng, g: eng.tensor_tensor(grp(dst, g), grp(a, g), grp(b, g), op))


def scale_heads_step(name, dst, src, factor, heads, after):
    n = GROUP * heads

    def f(eng, g):
        s = grp(factor, g, n).rearrange("p (m o) -> p m o", o=1).to_broadcast([P, n, D // heads])
        return eng.tensor_tensor(grp(dst, g).rearrange("p (m d) -> p m d", m=n),
                                 grp(src, g).rearrange("p (m d) -> p m d", m=n), s, ALU.mult)
    return (name, "vector", after, f)


def leaky_step(name, dst, src, after):
    return (name, "vector", after, lambda eng, g: eng.scalar_tensor_tensor(
        out=grp(dst, g), in0=grp(src, g), scalar=SLOPE, in1=grp(src, g), op0=ALU.mult, op1=ALU.max))


def layernorm_steps(B, name, dst, src, after, gamma=None, beta=None):
    st, mv, rs = B.ln_stats, B.ln_mean_var, B.ln_rstd

    def stats(eng, g):
        for k in range(GROUP):
            ins = eng.bn_stats(st[:, bass.ds((g * GROUP + k) * 6, 6)], src[:, bass.ds(g * WIDE + k * D, D)])
        return ins

    def aggregate(eng, g):
        for k in range(GROUP):
            ins = eng.bn_aggr(mv[:, bass.ds((g * GROUP + k) * 2, 2)], st[:, bass.ds((g * GROUP + k) * 6, 6)])
        return ins

    def root(eng, g):
        var = grp(mv, g, GROUP * 2).rearrange("p (k c) -> p k c", c=2)[:, :, 1]
        return eng.activation(grp(rs, g, GROUP), var, ACT.Sqrt, bias=B.eps[:, 0:1])

    def inverse(eng, g):
        return eng.reciprocal(grp(rs, g, GROUP), grp(rs, g, GROUP))

    def block_of(g, k):
        return (bass.ds(g * WIDE + k * D, D), mv[:, bass.ds((g * GROUP + k) * 2, 1)],
                rs[:, bass.ds(g * GROUP + k, 1)])

    def normalise(eng, g):
        for k in range(GROUP):
            c, mean, rstd = block_of(g, k)
            ins = eng.tensor_scalar(dst[:, c], src[:, c], mean, rstd, ALU.subtract, ALU.mult)
        return ins

    def centre(eng, g):
        for k in range(GROUP):
            c, mean, _ = block_of(g, k)
            ins = eng.scalar_tensor_tensor(out=dst[:, c], in0=src[:, c], scalar=mean, in1=gamma[:, :],
                                           op0=ALU.subtract, op1=ALU.mult)
        return ins

    def scale(eng, g):
        for k in range(GROUP):
            c, _, rstd = block_of(g, k)
            ins = eng.scalar_tensor_tensor(out=dst[:, c], in0=dst[:, c], scalar=rstd, in1=beta[:, :],
                                           op0=ALU.mult, op1=ALU.add)
        return ins
    steps = [(name + ".stats", "vector", after, stats),
             (name + ".aggr", "vector", [name + ".stats"], aggregate),
             (name + ".root", "scalar", [name + ".aggr"], root)]
    inv = (name + ".inv", "vector", [name + ".root"], inverse)
    if gamma is None:
        steps += [inv, (name, "vector", [name + ".inv"] + list(after), normalise)]
    else:
        steps += [(name + ".centred", "vector", [name + ".aggr"], centre), inv,
                  (name, "vector", [name + ".centred", name + ".inv"], scale)]
    return steps


def load(B, pairs):
    landed = B.count("load")
    with B.nc.Block() as block:
        @block.sync
        def _(eng):
            for dst, src in pairs:
                eng.dma_start(dst, src, allow_slow_non_contiguous=True).then_inc(landed.sem, 16)
            eng.wait_ge(landed.sem, landed.at(16 * len(pairs)))
    landed.advance(16 * len(pairs))


def store(B, pairs):
    load(B, pairs)


def turn_weights(B, pairs):
    pe, act = B.count("turn_pe"), B.count("turn_act")
    with B.nc.Block() as block:
        @block.tensor
        def _(eng):
            for j, (_, src) in enumerate(pairs):
                eng.transpose(B.ps[:, j * 512:j * 512 + D], src, B.ident[:, :]).then_inc(pe.sem, 1)

        @block.scalar
        def _(eng):
            for j, (dst, _) in enumerate(pairs):
                eng.wait_ge(pe.sem, pe.at(j + 1))
                eng.activation(dst, B.ps[:, j * 512:j * 512 + D], ACT.Copy).then_inc(act.sem, 1)
    pe.advance(len(pairs))
    act.advance(len(pairs))



def backwards(row):
    return row[:, ::-1]


def sort_edges_if_needed(B, tab, dst_f, step_f, ones):
    nc = B.nc
    slots = EDGES_PER_ROW * P
    keys = NODES_PAD // P
    counters = B.dram("counters", [NODES_PAD + P, 1])
    placed = {k: B.dram("placed_" + k, [slots, 1], ap.dtype) for k, ap in tab.items()}
    ve, pe, dma = B.count("edge_ve"), B.count("edge_pe"), B.count("edge_dma")
    token, wait_holder = B.count("sort_token").sem, B.count("sort_wait_holder").sem
    moved_in = [B.count(f"sort_moved{j}").sem for j in range(5)]

    with ExitStack() as ctx:
        follow = B.sb(ctx, "follow", [P, EDGES_PER_ROW], I32)
        falls = B.sb(ctx, "falls", [P, EDGES_PER_ROW])
        n_falls = B.sb(ctx, "n_falls", [P, 1])
        flag = B.sb(ctx, "flag", [P, 1], I32)
        before, after = B.sb(ctx, "before", [P, P]), B.sb(ctx, "after", [P, P])
        row_i = B.sb(ctx, "row_i", [P, P], I32)
        row, same, part = (B.sb(ctx, n, [P, P]) for n in ("row", "same", "part"))
        col = {k: B.sb(ctx, "col_" + k, [P, 1], ap.dtype) for k, ap in tab.items()}
        edge_p, key, count, rank, total, later, place = (
            B.sb(ctx, n, [P, 1]) for n in ("edge_p", "key", "count", "rank", "total", "later", "place"))
        key_i, place_i, counter_i = (B.sb(ctx, n, [P, 1], I32) for n in ("key_i", "place_i", "counter_i"))
        hist, incl = B.sb(ctx, "hist", [P, keys]), B.sb(ctx, "incl", [P, keys])
        zero = B.sb(ctx, "zero_row", [P, keys + 1])
        copy = {k: B.sb(ctx, "copy_" + k, [P, EDGES_PER_ROW], ap.dtype) for k, ap in tab.items()}

        with nc.Block() as block:
            @block.sync
            def _(eng):
                eng.wait_ge(ve.sem, ve.at(1))
                flat = tab["dst"].tensor
                eng.dma_start(follow[0:P - 1, :], bass.AP(tensor=flat, offset=1, ap=[[EDGES_PER_ROW, P - 1], [1, EDGES_PER_ROW]])
                              ).then_inc(dma.sem, 16)
                eng.dma_start(follow[P - 1:P, 0:EDGES_PER_ROW - 1],
                              bass.AP(tensor=flat, offset=1 + (P - 1) * EDGES_PER_ROW,
                                      ap=[[EDGES_PER_ROW, 1], [1, EDGES_PER_ROW - 1]])).then_inc(dma.sem, 16)

            @block.vector
            def _(eng):
                link = Chain(eng, ve)
                link(eng.memset(follow[:, :], NO_NODE))
                eng.memset(zero[:, :], 0.0)
                eng.wait_ge(dma.sem, dma.at(32))
                link(eng.tensor_tensor(falls[:, :], follow[:, :], dst_f[:, :], ALU.is_lt))
                link(eng.tensor_reduce(n_falls[:, :], falls[:, :], X_AXIS, ALU.add))
                eng.tensor_copy(edge_p[:, :], step_f[:, 0:1])
                eng.tensor_scalar(before[:, :], B.iota[:, :], step_f[:, 0:1], None, ALU.is_lt)
                eng.tensor_scalar(after[:, :], B.iota[:, :], step_f[:, 0:1], None, ALU.is_gt)
                eng.wait_ge(pe.sem, pe.at(1))
                link(eng.tensor_scalar(flag[:, :], B.ps[:, 0:1], 1.0, None, ALU.min))

            @block.tensor
            def _(eng):
                eng.wait_ge(ve.sem, ve.at(3))
                eng.matmul(B.ps[:, 0:1], ones[:, :], n_falls[:, :], start=True, stop=True).then_inc(pe.sem, 1)
        ve.advance(4)
        pe.advance(1)
        dma.advance(32)

        def tt(dst, a, b, op):
            return ("vector", 1, lambda e, c: e.tensor_tensor(dst[:, :], a[:, :], b[:, :], op))

        def ts(dst, a, s1, s2, op1, op2=None):
            return ("vector", 1, lambda e, c: e.tensor_scalar(dst[:, :], a[:, :], s1, s2, op1, *([op2] if op2 else [])))

        def total_of(dst, src):
            return ("vector", 1, lambda e, c: e.tensor_reduce(dst[:, :], src[:, :], X_AXIS, ALU.add))

        def dma_step(make):
            return ("sync", 16, lambda e, c: e.dma_start(*make(c), allow_slow_non_contiguous=True))

        def scatter(table, index, src):
            return ("gpsimd", 1, lambda e, c: e.indirect_dma_start(
                table[:, :], bass.IndirectOffsetOnAxis(ap=index[:, 0:1], axis=0), src[:, :], None))

        def chunk_of(k, c):
            return tab[k][bass.ds(c, 1), :]

        count_steps = [
            dma_step(lambda c: (row_i[:, :], chunk_of("dst", c).to_broadcast([P, P]))),
            dma_step(lambda c: (col["dst"][:, :], chunk_of("dst", c).rearrange("o p -> p o"))),
            ts(row, row_i, float(N_NODES), None, ALU.min),
            ts(key, col["dst"], float(N_NODES), None, ALU.min),
            ts(key_i, key, 1.0, None, ALU.mult),
            ("gpsimd", 1, lambda e, c: e.indirect_dma_start(
                count[:, :], None, counters[:, :], bass.IndirectOffsetOnAxis(ap=key_i[:, 0:1], axis=0))),
            ("vector", 1, lambda e, c: e.tensor_scalar(same[:, :], row[:, :], key[:, 0:1], None, ALU.is_equal)),
            tt(part, same, before, ALU.mult), total_of(rank, part),
            tt(part, same, after, ALU.mult), total_of(later, part), total_of(total, same),
            tt(place, count, rank, ALU.add), ts(place_i, place, 1.0, None, ALU.mult),
            tt(count, count, total, ALU.add),
            ts(later, later, 1.0, None, ALU.min),
            tt(total, edge_p, key, ALU.subtract), ts(total, total, float(NODES_PAD), None, ALU.add),
            tt(total, total, later, ALU.mult), tt(total, total, key, ALU.add),
            ts(counter_i, total, 1.0, None, ALU.mult),
            scatter(counters, counter_i, count)]
        place_steps = [dma_step(lambda c: (col["src"][:, :], chunk_of("src", c).rearrange("o p -> p o"))),
                       dma_step(lambda c: (col["w"][:, :], chunk_of("w", c).rearrange("o p -> p o")))]
        place_steps += [scatter(placed[k], place_i, col[k]) for k in tab]
        counters_sb = counters[0:NODES_PAD, :].rearrange("(p k) o -> p (k o)", p=P)
        clear = [dma_step(lambda c: (counters_sb, zero[:, 0:keys])),
                 dma_step(lambda c: (counters[NODES_PAD:, :], zero[:, keys:keys + 1]))]
        starts = [
            dma_step(lambda c: (hist[:, :], counters_sb)),
            ("vector", 1, lambda e, c: e.tensor_tensor_scan(incl[:, :], hist[:, :], zero[:, 0:keys], 0.0, ALU.add, ALU.add)),
            ("tensor", 1, lambda e, c: e.matmul(B.ps[:, 0:1], after[:, :], incl[:, keys - 1:keys], start=True, stop=True)),
            tt(incl, incl, hist, ALU.subtract),
            ("vector", 1, lambda e, c: e.tensor_copy(rank[:, :], B.ps[:, 0:1])),
            ("vector", 1, lambda e, c: e.tensor_scalar(incl[:, :], incl[:, :], rank[:, 0:1], None, ALU.add)),
            dma_step(lambda c: (counters_sb, incl[:, :]))]
        back = [dma_step(lambda c, k=k: (copy[k][:, :], placed[k].rearrange("(p j) o -> p (j o)", p=P))) for k in tab]
        back += [dma_step(lambda c, k=k: (bass.AP(tensor=tab[k].tensor, offset=0,
                                                  ap=[[EDGES_PER_ROW, P], [1, EDGES_PER_ROW]]), copy[k][:, :])) for k in tab]
        phases = [(clear, 1), (count_steps, TABLE_CHUNKS), (starts, 1), (count_steps + place_steps, TABLE_CHUNKS), (back, 1)]

        def program(which):
            def run(eng):
                unsorted = eng.value_load(flag[0:1, 0:1], min_val=0, max_val=1)
                with eng.If(unsorted):
                    if which == "vector":
                        eng.sem_inc(token, 1)
                    at = 1
                    for moved, (steps, turns) in zip(moved_in, phases):
                        per = sum(n for _, n, _ in steps)
                        moves_per = sum(16 for e, _, _ in steps if e == "gpsimd")

                        def turn(c):
                            done, m = at, 0
                            for e, n, emit in steps:
                                if e == which:
                                    eng.wait_ge(token, c * per + done)
                                if e == which == "gpsimd":
                                    eng.sem_inc(wait_holder, 1)
                                    m += 16
                                    emit(eng, c).then_inc(moved, 16)
                                    eng.wait_ge(moved, c * moves_per + m)
                                    eng.sem_inc(token, 1)
                                elif e == which:
                                    emit(eng, c).then_inc(token, n)
                                done += n
                        if turns == 1:
                            turn(0)
                        else:
                            with eng.Fori(0, turns) as c:
                                turn(c)
                        at += per * turns
                    eng.wait_ge(token, at)
            return run

        with nc.Block() as block:
            block.gpsimd(program("gpsimd"))
            block.vector(program("vector"))
            block.tensor(program("tensor"))
            block.sync(program("sync"))


def lay_out_edges(B):
    nc = B.nc
    ins = B.ins
    tab = {k: B.dram("tab_" + k, [TABLE_CHUNKS, P], dt)
           for k, dt in (("src", I32), ("dst", I32), ("w", F32))}
    block_of_step = B.dram("block_of_step", [STEPS_PAD], F32)
    L = STEPS * P
    B.keys = B.dram("keys", [L + 2, 1])
    keys = B.keys.tensor
    flat = {"src": ins["src"], "dst": ins["dst"], "w": ins["edge_weight"]}

    with ExitStack() as ctx:
        full = {k: B.sb(ctx, "full_" + k, [P, EDGES_PER_ROW], F32 if k == "w" else I32) for k in tab}
        dst_f = B.sb(ctx, "dst_f", [P, EDGES_PER_ROW])
        junk = B.sb(ctx, "junk", [P, EDGES_PER_ROW])
        edge_of_block = B.sb(ctx, "edge_of_block", [P, BLOCKS - 1])
        below = B.sb(ctx, "below", [P, BLOCKS - 1])
        start_i = B.sb(ctx, "start_i", [P, BLOCKS - 1], I32)
        first_step = B.sb(ctx, "first_step", [P, BLOCKS - 1])
        iota_i = B.sb(ctx, "iota_i", [P, P], I32)
        step_i = B.sb(ctx, "step_i", [P, STEP_COLS], I32)
        block_i = B.sb(ctx, "block_i", [P, BLOCKS - 1], I32)
        step_f = B.sb(ctx, "step_f", [P, STEP_COLS])
        entered = B.sb(ctx, "entered", [P, STEP_COLS, BLOCKS - 1])
        block_f = B.sb(ctx, "block_f", [P, STEP_COLS])
        base_f = B.sb(ctx, "base_f", [P, STEP_COLS])
        chunk_f = B.sb(ctx, "chunk_f", [P, STEP_COLS])
        chunk_i = B.sb(ctx, "chunk_i", [P, STEP_COLS], I32)
        rows = {k: B.sb(ctx, "rows_" + k, [P, STEP_COLS, P], F32 if k == "w" else I32) for k in tab}
        src_f = B.sb(ctx, "src_f", [P, STEP_COLS, P])
        local = B.sb(ctx, "local", [P, STEP_COLS, P])
        key = B.sb(ctx, "key", [P, STEP_COLS, P])
        key_next = B.sb(ctx, "key_next", [P, STEP_COLS, P])
        halo = B.sb(ctx, "halo", [1, 2])
        reg_f = B.sb(ctx, "reg_f", [1, STEPS_PAD])
        far = B.sb(ctx, "far", [1, STEPS_PAD])
        ones = B.sb(ctx, "ones", [P, P])

        ve, po, pe, dma = (B.count(n) for n in ("edge_ve", "edge_po", "edge_pe", "edge_dma"))
        gat = B.count("edge_gather")
        dst_in = B.count("edge_dst")
        act = B.count("edge_act")
        kept = [B.count(f"kept{q}") for q in range(BODY_GROUPS)]

        with nc.Block() as block:
            @block.vector
            def _(eng):
                eng.memset(full["src"][:, :], 0)
                eng.memset(full["dst"][:, :], NO_NODE)
                eng.memset(full["w"][:, :], 0.0)
                eng.memset(ones[:, :], 1.0)
                eng.memset(B.x[:, :], 0.0)
                eng.memset(B.eps[:, :], LN_EPS)
                eng.memset(B.zeros[:, :], 0.0)
                eng.memset(halo[:, 0:1], BIG)
                eng.memset(halo[:, 1:2], -2.0 * NO_NODE * BIG)
                eng.memset(B.ident[:, :], 0.0).then_inc(ve.sem, 1)

            @block.gpsimd
            def _(eng):
                eng.iota(iota_i[:, :], [[1, P]], base=0, channel_multiplier=0)
                eng.iota(step_i[:, :], [[P, STEP_COLS]], base=0, channel_multiplier=1)
                eng.iota(block_i[:, :], [[1, BLOCKS - 1]], base=1, channel_multiplier=0)
                eng.wait_ge(ve.sem, ve.at(1))
                eng.affine_select(out=B.ident[:, :], in_=B.ident[:, :], compare_op=ALU.not_equal, fill=1.0,
                                  base=0, pattern=[[-1, P]], channel_multiplier=1)
        ve.advance(1)

        with nc.Block() as block:
            @block.sync
            def _(eng):
                n = 0
                for k in ("dst", "src", "w"):
                    t, v = full[k], flat[k]
                    here = dst_in if k == "dst" else dma
                    eng.dma_start(t[0:FULL_ROWS, :], v[0:FULL_ROWS * EDGES_PER_ROW].rearrange(
                        "(p j) -> p j", j=EDGES_PER_ROW)).then_inc(here.sem, 16)
                    eng.dma_start(t[FULL_ROWS:FULL_ROWS + 1, 0:LAST_EDGES],
                                  v[FULL_ROWS * EDGES_PER_ROW:N_EDGES].rearrange(
                                      "(p j) -> p j", p=1)).then_inc(here.sem, 16)
                    if here is dma:
                        n += 2
                eng.dma_start(over_groups(B.x[:, 0:FULL_BLOCKS * D]),
                              ins["x"][0:FULL_BLOCKS * P, :].rearrange("(b p) d -> p b d", p=P)
                              ).then_inc(dma.sem, 16)
                eng.dma_start(B.x[0:LAST_NODES, FULL_BLOCKS * D:(FULL_BLOCKS + 1) * D],
                              ins["x"][FULL_BLOCKS * P:N_NODES, :]).then_inc(dma.sem, 16)
                n += 2
                eng.wait_ge(dst_in.sem, dst_in.at(32))
                eng.wait_ge(dma.sem, dma.at(16 * n))
                for q, (k, t) in enumerate(full.items()):
                    whole = bass.AP(tensor=tab[k].tensor, offset=0, ap=[[EDGES_PER_ROW, P], [1, EDGES_PER_ROW]])
                    eng.dma_start(whole, t[:, :]).then_inc(kept[q].sem, 16)
                eng.dma_start(bass.AP(tensor=keys, offset=0, ap=[[1, 1], [1, 1]]), halo[:, 0:1]).then_inc(kept[3].sem, 16)
                eng.dma_start(bass.AP(tensor=keys, offset=L + 1, ap=[[1, 1], [1, 1]]), halo[:, 1:2]).then_inc(dma.sem, 16)
                n += 1
                eng.wait_ge(dma.sem, dma.at(16 * n))
                for c in kept:
                    eng.wait_ge(c.sem, c.at(16))

            @block.vector
            def _(eng):
                link = Chain(eng, ve)
                eng.wait_ge(dst_in.sem, dst_in.at(32))
                link(eng.tensor_copy(dst_f[:, :], full["dst"][:, :]))
                eng.tensor_copy(B.iota[:, :], iota_i[:, :])
                eng.tensor_copy(step_f[:, :], step_i[:, :])
                link(eng.tensor_copy(edge_of_block[:, :], block_i[:, :]))
                link(eng.tensor_scalar(first_step[:, :], edge_of_block[:, :], float(P), None, ALU.mult))
                with eng.Fori(0, BLOCKS - 1) as b:
                    eng.wait_ge(ve.sem, ve.at(3) + b)
                    eng.tensor_scalar(junk[:, :], dst_f[:, :], first_step[:, bass.ds(b, 1)], 0.0, ALU.is_lt,
                                      ALU.add, accum_out=below[:, bass.ds(b, 1)]).then_inc(ve.sem, 1)
                eng.wait_ge(pe.sem, pe.at(1))
                link.n += BLOCKS - 1
                link(eng.tensor_copy(start_i[:, :], B.ps[:, 0:BLOCKS - 1]))
                link(eng.tensor_scalar(start_i[:, :], start_i[:, :], 7, None, ALU.arith_shift_right))
                link(eng.tensor_copy(first_step[:, :], start_i[:, :]))
                link(eng.tensor_tensor(first_step[:, :], first_step[:, :], edge_of_block[:, :], ALU.add))
                link(eng.tensor_tensor(
                    entered[:, :, :],
                    first_step[:, :].rearrange("p (o b) -> p o b", o=1).to_broadcast([P, STEP_COLS, BLOCKS - 1]),
                    step_f[:, :].rearrange("p (s o) -> p s o", o=1).to_broadcast([P, STEP_COLS, BLOCKS - 1]),
                    ALU.is_le))
                link(eng.tensor_reduce(block_f[:, :], entered[:, :, :], X_AXIS, ALU.add))
                link(eng.tensor_tensor(chunk_f[:, :], step_f[:, :], block_f[:, :], ALU.subtract))
                link(eng.tensor_scalar(chunk_f[:, :], chunk_f[:, :], float(TABLE_CHUNKS - 1), None, ALU.min))
                link(eng.tensor_copy(chunk_i[:, :], chunk_f[:, :]))
                link(eng.tensor_scalar(base_f[:, :], block_f[:, :], float(P), None, ALU.mult))

            @block.tensor
            def _(eng):
                eng.wait_ge(ve.sem, ve.at(3 + BLOCKS - 1))
                eng.matmul(B.ps[:, 0:BLOCKS - 1], ones[:, :], below[:, :], start=True, stop=True).then_inc(pe.sem, 1)
        dst_in.advance(32)
        dma.advance(16 * (2 * 2 + 2 + 1))
        for c in kept:
            c.advance(16)
        ve.advance(3 + BLOCKS - 1 + 10)
        pe.advance(1)

        sort_edges_if_needed(B, tab, dst_f, step_f, ones)

        with nc.Block() as block:
            @block.gpsimd
            def _(eng):
                n = 0
                for k in tab:
                    for c in range(STEP_COLS):
                        eng.indirect_dma_start(rows[k][:, c, :], None, tab[k][:, :],
                                               bass.IndirectOffsetOnAxis(ap=chunk_i[:, c:c + 1], axis=0)
                                               ).then_inc(gat.sem, 16)
                        n += 1
                eng.dma_start(block_of_step.rearrange("(c p) -> p c", p=P), block_f[:, :],
                              allow_slow_non_contiguous=True).then_inc(gat.sem, 16)
                n += 1
                eng.wait_ge(gat.sem, gat.at(16 * n))
        gat.advance(16 * (3 * STEP_COLS + 1))

        with nc.Block() as block:
            @block.sync
            def _(eng):
                eng.dma_start(reg_f[:, :], block_of_step.rearrange("(o s) -> o s", o=1)).then_inc(dma.sem, 16)
                eng.wait_ge(ve.sem, ve.at(4))
                for c in range(STEP_COLS):
                    m = min(P, STEPS - c * P)
                    eng.dma_start(bass.AP(tensor=keys, offset=1 + c * P * P, ap=[[P, m], [1, P]]),
                                  key[0:m, c, :]).then_inc(dma.sem, 16)
                eng.wait_ge(dma.sem, dma.at(16 * (1 + STEP_COLS)))
                for c in range(STEP_COLS):
                    m = min(P, STEPS - c * P)
                    eng.dma_start(key_next[0:m, c, :],
                                  bass.AP(tensor=keys, offset=2 + c * P * P, ap=[[P, m], [1, P]])).then_inc(dma.sem, 16)

            @block.vector
            def _(eng):
                link = Chain(eng, ve)
                eng.tensor_copy(src_f[:, :, :], rows["src"][:, :, :])
                eng.memset(key_next[:, :, :], 0.0)
                base = base_f[:, :].rearrange("p (c o) -> p c o", o=1).to_broadcast([P, STEP_COLS, P])
                link(eng.tensor_tensor(local[:, :, :], rows["dst"][:, :, :], base, ALU.subtract))
                link(eng.tensor_scalar(local[:, :, :], local[:, :, :], -0.5, P - 0.5, ALU.max, ALU.min))
                link(eng.tensor_tensor(key[:, :, :], local[:, :, :], base, ALU.add))
                link(eng.tensor_scalar(key[:, :, :], key[:, :, :], -BIG, None, ALU.mult))
                eng.wait_ge(dma.sem, dma.at(16 * (1 + 2 * STEP_COLS)))
                link(eng.tensor_tensor(key_next[:, :, :], key[:, :, :], key_next[:, :, :], ALU.not_equal))
                columns = B.columns[:, :].rearrange("p (i c s) -> p i c s", c=2, s=BODY)
                of_block = reg_f[:, 0:STEPS].rearrange("p (i s) -> p i s", s=BODY)
                beyond = far[:, 0:STEPS].rearrange("p (i s) -> p i s", s=BODY)
                link(eng.tensor_scalar(columns[:, :, 0, :], of_block, float(D), None, ALU.mult))
                link(eng.tensor_scalar(beyond, of_block, float(EXTRA_SPLIT),
                                       float(EXTRA_REST_AT - EXTRA_AT - EXTRA_SPLIT * PART_COLS), ALU.is_ge, ALU.mult))
                link(eng.tensor_scalar(of_block, of_block, float(PART_COLS), float(EXTRA_AT), ALU.mult, ALU.add))
                link(eng.tensor_tensor(columns[:, :, 1, :], of_block, beyond, ALU.add))

            @block.tensor
            def _(eng):
                eng.wait_ge(ve.sem, ve.at(2))
                for j, t in enumerate((src_f, local, rows["w"])):
                    if j == 2:
                        eng.wait_ge(act.sem, act.at(1))
                    for c in range(STEP_COLS):
                        at = (j % 2) * 1024 + c * P
                        ins = eng.transpose(B.ps[:, at:at + P], t[:, c, :], B.ident[:, :])
                    ins.then_inc(pe.sem, 1)
                eng.wait_ge(act.sem, act.at(2))
                eng.wait_ge(ve.sem, ve.at(5))
                for c in range(STEP_COLS):
                    ins = eng.transpose(B.ps[:, 1024 + c * P:1024 + (c + 1) * P], key_next[:, c, :], B.ident[:, :])
                ins.then_inc(pe.sem, 1)

            @block.scalar
            def _(eng):
                for j, t in enumerate((B.edge_src, B.edge_local, B.edge_weight, B.edge_last)):
                    eng.wait_ge(pe.sem, pe.at(j + 1))
                    at = (j % 2) * 1024
                    eng.activation(t[:, :], B.ps[:, at:at + STEPS_PAD], ACT.Copy).then_inc(act.sem, 1)
        ve.advance(9)
        dma.advance(16 * (1 + 2 * STEP_COLS))
        pe.advance(4)
        act.advance(4)



def one_hot(B, eng, dst, step):
    loc = B.edge_local[:, bass.ds(step, GROUP)].rearrange("p (k o) -> p k o", o=1).to_broadcast([P, GROUP, P])
    io = B.iota[:, :].rearrange("p (o n) -> p o n", o=1).to_broadcast([P, GROUP, P])
    return eng.tensor_tensor(dst, io, loc, ALU.is_equal)


class ColumnRegisters:

    def __init__(self, B, eng, with_extras=False):
        self.B, self.eng, self.tables = B, eng, 2 if with_extras else 1
        self.regs = [eng.alloc_register(f"column{B.fresh()}") for j in range(self.tables * BODY)]

    def load(self, turn):
        self.eng.load(self.regs, self.B.columns[0:1, bass.ds(turn * (2 * BODY), self.tables * BODY)])
        top = (BLOCKS - 1) * D, COLUMNS - PART_WIDE
        values = [self.eng.snap(r, donate=True, min_val=0, max_val=top[j // BODY]) for j, r in enumerate(self.regs)]
        return values[:BODY], values[BODY:]

    def free(self):
        for r in self.regs:
            self.eng.free_register(r)


def gather_rows(B, eng, slots, table, width, s, sems):
    eng.indirect_dma_start(slots[:, s * width:(s + 1) * width], None, table,
                           bass.IndirectOffsetOnAxis(ap=B.index_ring[:, s:s + 1], axis=0)
                           ).then_inc(sems[s].sem, 16)


def clear_sums(B, eng):
    for b in range(8):
        eng.matmul(B.bank(b), B.zeros[:, 0:P], B.zeros[:, :], start=True, stop=True, skip_group_check=True)


def gcn_pass(B, table):
    nc = B.nc
    with ExitStack() as ctx:
        rows = B.sb(ctx, "gcn_rows", [P, BODY * D])
        hot = B.sb(ctx, "gcn_hot", [P, BODY, P])
        landed = [B.count(f"gather{s}") for s in range(BODY)]
        index, hot_made, used = (B.count(n) for n in ("index", "hot", "used"))
        wait_holder = B.count("wait_holder")
        with nc.Block() as block:
            @block.scalar
            def _(eng):
                with eng.Fori(0, TURNS) as i:
                    for h in range(2):
                        eng.wait_ge(used.sem, used.at(h + 1) + i * 2)
                        eng.activation(B.index_ring[:, h * HALF:(h + 1) * HALF],
                                       B.edge_src[:, bass.ds(i * BODY + h * HALF, HALF)], ACT.Copy
                                       ).then_inc(index.sem, 1)

            @block.gpsimd
            def _(eng):
                with eng.Fori(0, TURNS) as i:
                    for h in range(2):
                        eng.wait_ge(index.sem, index.at(h + 1) + i * 2)
                        eng.sem_inc(wait_holder.sem, 1)
                        for s in range(h * HALF, (h + 1) * HALF):
                            gather_rows(B, eng, rows, table, D, s, landed)

            @block.vector
            def _(eng):
                with eng.Fori(0, TURNS) as i:
                    for h in range(2):
                        eng.wait_ge(used.sem, used.at(h + 1) + i * 2)
                        for s in range(h * HALF, (h + 1) * HALF):
                            t = i * BODY + s
                            ins = eng.tensor_scalar(hot[:, s, :], B.iota[:, :], B.edge_local[:, bass.ds(t, 1)],
                                                    B.edge_weight[:, bass.ds(t, 1)], ALU.is_equal, ALU.mult)
                        ins.then_inc(hot_made.sem, 1)

            @block.tensor
            def _(eng):
                eng.sem_inc(used.sem, 2)
                clear_sums(B, eng)
                columns = ColumnRegisters(B, eng)
                with eng.Fori(0, TURNS) as i:
                    sum_at, _ = columns.load(i)
                    for h in range(2):
                        eng.wait_ge(hot_made.sem, hot_made.at(h + 1) + i * 2)
                        for k in range(HALF):
                            s = h * HALF + k
                            eng.wait_ge(landed[s].sem, landed[s].at(16) + i * 16)
                            ins = eng.matmul(B.ps[:, bass.ds(sum_at[s], D)], hot[:, s, :],
                                             rows[:, s * D:(s + 1) * D], start=False, stop=True,
                                             skip_group_check=True)
                        ins.then_inc(used.sem, 1)
                columns.free()
        for c in landed:
            c.advance(16 * TURNS)
        index.advance(2 * TURNS)
        hot_made.advance(2 * TURNS)
        used.advance(2 * TURNS + 2)


def score_pass(B, table, width, heads, queries, att, logits):
    nc = B.nc
    dim = D // heads
    with ExitStack() as ctx:
        rows = B.sb(ctx, "rows", [P, BODY * width])
        hot = B.sb(ctx, "hot", [P, 2, GROUP, P])
        hot_t = B.sb(ctx, "hot_t", [P, 2, GROUP * P])
        z = B.sb(ctx, "z", [P, 2, WIDE])
        landed = [B.count(f"gather{s}") for s in range(BODY)]
        kept = [B.count(f"kept{q}") for q in range(BODY_GROUPS)]
        index, hot_made, turned, hot_kept, asked, zed = (
            B.count(n) for n in ("index", "hot", "turned", "hot_kept", "asked", "zed"))
        wait_holder = B.count("wait_holder")
        per = 2 if att is None else 4

        def group_rows(q, lo):
            return rows[:, q * GROUP * width:(q + 1) * GROUP * width].rearrange(
                "p (k w) -> p k w", w=width)[:, :, lo:lo + D]

        with nc.Block() as block:
            @block.gpsimd
            def _(eng):
                with eng.Fori(0, TURNS) as i:
                    for h in range(2):
                        eng.wait_ge(index.sem, index.at(h + 1) + i * 2)
                        for q in range(2 * h, 2 * h + 2):
                            eng.wait_ge(kept[q].sem, kept[q].at(0) + i * 16)
                            eng.sem_inc(wait_holder.sem, 1)
                            for s in range(q * GROUP, (q + 1) * GROUP):
                                gather_rows(B, eng, rows, table, width, s, landed)

            @block.sync
            def _(eng):
                with eng.Fori(0, TURNS) as i:
                    for q in range(BODY_GROUPS):
                        for s in range(q * GROUP, (q + 1) * GROUP):
                            eng.wait_ge(landed[s].sem, landed[s].at(16) + i * 16)
                        eng.dma_start(over_groups(B.spool[bass.ds((i * BODY_GROUPS + q) * P, P), :]),
                                      group_rows(q, width - D)).then_inc(kept[q].sem, 16)
                for q in range(BODY_GROUPS):
                    eng.wait_ge(kept[q].sem, kept[q].at(16 * TURNS))

            @block.scalar
            def _(eng):
                with eng.Fori(0, TURNS) as i:
                    for q in range(BODY_GROUPS):
                        if q % 2 == 0:
                            h = q // 2
                            eng.wait_ge(zed.sem, zed.at((2 * h + 2) * per) + i * (BODY_GROUPS * per))
                            eng.activation(B.index_ring[:, h * HALF:(h + 1) * HALF],
                                           B.edge_src[:, bass.ds(i * BODY + h * HALF, HALF)], ACT.Copy
                                           ).then_inc(index.sem, 1)
                        n = i * BODY_GROUPS + q
                        eng.wait_ge(turned.sem, turned.at(3) + n)
                        eng.wait_ge(asked.sem, asked.at(1) + n)
                        eng.activation(hot_t[:, q % 2, :], B.bank(q % 2), ACT.Copy).then_inc(hot_kept.sem, 1)

            @block.vector
            def _(eng):
                eng.sem_inc(zed.sem, BODY_GROUPS * per)

                def make_hot(n, slot):
                    eng.wait_ge(turned.sem, turned.at(1) + n)
                    one_hot(B, eng, hot[:, slot, :, :], n * GROUP).then_inc(hot_made.sem, 1)

                make_hot(0, 0)
                with eng.Fori(0, TURNS) as i:
                    for q in range(BODY_GROUPS):
                        n = i * BODY_GROUPS + q
                        make_hot(n + 1, (q + 1) % 2)
                        eng.wait_ge(asked.sem, asked.at(3) + n)
                        for s in range(q * GROUP, (q + 1) * GROUP):
                            eng.wait_ge(landed[s].sem, landed[s].at(16) + i * 16)
                        zz = z[:, q % 2, :]
                        query = B.bank(2 + q % 2)
                        done = zed.at(BODY_GROUPS * per) + n * per

                        def then(j, ins):
                            ins.then_inc(zed.sem, 1)
                            eng.wait_ge(zed.sem, done + (j + 1))
                        out = logits[:, bass.ds(n * (GROUP * heads), GROUP * heads)]
                        if att is None:
                            then(0, eng.tensor_tensor(over_groups(zz), over_groups(query), group_rows(q, 0), ALU.mult))
                        else:
                            then(0, eng.tensor_tensor(over_groups(zz), over_groups(query), group_rows(q, 0), ALU.add))
                            then(1, eng.scalar_tensor_tensor(out=zz, in0=zz, scalar=SLOPE, in1=zz,
                                                             op0=ALU.mult, op1=ALU.max))
                            a = att[:, :].rearrange("p (o d) -> p o d", o=1).to_broadcast([P, GROUP, D])
                            then(2, eng.tensor_tensor(over_groups(zz), over_groups(zz), a, ALU.mult))
                        eng.tensor_reduce(out, zz.rearrange("p (m d) -> p m d", d=dim), X_AXIS, ALU.add
                                          ).then_inc(zed.sem, 1)

            @block.tensor
            def _(eng):
                eng.sem_inc(turned.sem, 2)
                eng.sem_inc(asked.sem, 2)
                columns = ColumnRegisters(B, eng)
                with eng.Fori(0, TURNS) as i:
                    sum_at, _ = columns.load(i)
                    for q in range(BODY_GROUPS):
                        n = i * BODY_GROUPS + q
                        eng.wait_ge(hot_made.sem, hot_made.at(1) + n)
                        for k in range(GROUP):
                            ins = eng.transpose(B.ps[:, (q % 2) * 512 + k * P:(q % 2) * 512 + (k + 1) * P],
                                                hot[:, q % 2, k, :], B.ident[:, :])
                        ins.then_inc(turned.sem, 1)
                        eng.wait_ge(hot_kept.sem, hot_kept.at(1) + n)
                        eng.wait_ge(zed.sem, zed.at((BODY_GROUPS - 1) * per) + n * per)
                        for k in range(GROUP):
                            at = (2 + q % 2) * 512 + k * D
                            ins = eng.matmul(B.ps[:, at:at + D], hot_t[:, q % 2, k * P:(k + 1) * P],
                                             queries[:, bass.ds(sum_at[q * GROUP + k], D)],
                                             start=True, stop=True)
                        ins.then_inc(asked.sem, 1)
                columns.free()
        for c in landed:
            c.advance(16 * TURNS)
        for c in kept:
            c.advance(16 * TURNS)
        index.advance(2 * TURNS)
        hot_made.advance(STEP_GROUPS + 1)
        turned.advance(STEP_GROUPS + 2)
        hot_kept.advance(STEP_GROUPS)
        asked.advance(STEP_GROUPS + 2)
        zed.advance((STEP_GROUPS + BODY_GROUPS) * per)


def segment_softmax(B, heads, scale, logits, extra, with_max):
    nc = B.nc
    slices = min(P // heads, 64)
    R = heads * slices
    per_slice = STEPS // slices
    L = per_slice * P
    batch = per_slice // 13
    n_batch = per_slice // batch
    BW = batch * P
    keys = B.keys.tensor
    with ExitStack() as ctx:
        lt = B.sb(ctx, "lt", [R, L])
        fw = B.sb(ctx, "fw", [R, L])
        key = B.sb(ctx, "keyrow", [R, L + 2])
        reset = B.sb(ctx, "reset", [R, L + 1], mybir.dt.bfloat16)
        ends = B.sb(ctx, "ends", [R, 4])
        end_keys = B.sb(ctx, "end_keys", [R, 2])
        row = B.sb(ctx, "row", [1, 4 * R + 1])
        open_f = B.sb(ctx, "open_f", [1, R + 1])
        open_b = B.sb(ctx, "open_b", [1, R + 1])
        pen = B.sb(ctx, "pen", [1, 2 * R])
        carry_row = B.sb(ctx, "carry_row", [1, 2 * R])
        carry = B.sb(ctx, "carry", [R, 2])
        stage = B.sb(ctx, "stage", [P, 2, batch * R])
        pe, act, ve, dma, staged = (B.count(n) for n in ("seg_pe", "seg_act", "seg_ve", "seg_dma", "seg_staged"))
        lg = logits[:, 0:STEPS * heads].rearrange("p (s t h) -> p t h s", s=slices, h=heads)
        ex = extra[:, :].rearrange("p (s t c) -> p t c s", s=slices, c=EXTRA)
        chain_n = 15
        ops = 2 if with_max else 1
        with nc.Block() as block:
            @block.sync
            def _(eng):
                for h in range(heads):
                    eng.dma_start(key[h * slices:(h + 1) * slices, :],
                                  bass.AP(tensor=keys, offset=0, ap=[[L, slices], [1, L + 2]])).then_inc(dma.sem, 16)

            @block.tensor
            def _(eng):
                for j in range(n_batch):
                    if j >= 7:
                        eng.wait_ge(act.sem, act.at(j - 6))
                    eng.wait_ge(staged.sem, staged.at(j + 1))
                    for m in range(batch):
                        at = (j % 7) * 512 + m * P
                        ins = eng.transpose(B.ps[0:R, at:at + P],
                                            stage[:, j % 2, m * R:(m + 1) * R], B.ident[:, :])
                    ins.then_inc(pe.sem, 1)
                eng.wait_ge(ve.sem, ve.at(4))
                eng.wait_ge(act.sem, act.at(n_batch))
                for c in range(4):
                    ins = eng.transpose(B.ps[0:1, c * 128:c * 128 + R], ends[:, c:c + 1], B.ident[0:R, 0:R])
                ins.then_inc(pe.sem, 1)
                eng.wait_ge(ve.sem, ve.at(12))
                for c in range(2):
                    ins = eng.transpose(B.ps[0:R, 512 + c:512 + c + 1], carry_row[:, c * R:(c + 1) * R],
                                        B.ident[0:1, 0:1])
                ins.then_inc(pe.sem, 1)
                eng.wait_ge(ve.sem, ve.at(chain_n))
                for j in range(n_batch):
                    if j >= 7:
                        eng.wait_ge(ve.sem, ve.at(chain_n + (j - 6) * ops))
                    for m in range(batch):
                        at = (j % 7) * 512 + m * P
                        g = j * batch + m
                        ins = eng.transpose(B.ps[:, at:at + R], lt[:, g * P:(g + 1) * P], B.ident[0:R, 0:R])
                    ins.then_inc(pe.sem, 1)

            @block.scalar
            def _(eng):
                for j in range(n_batch):
                    eng.wait_ge(pe.sem, pe.at(j + 1))
                    eng.activation(lt[:, j * BW:(j + 1) * BW], B.ps[0:R, (j % 7) * 512:(j % 7) * 512 + BW],
                                   ACT.Copy).then_inc(act.sem, 1)
                eng.wait_ge(ve.sem, ve.at(4))
                eng.activation(fw[:, :], key[:, 1:L + 1], ACT.Identity, bias=end_keys[:, 0:1]).then_inc(act.sem, 1)
                eng.wait_ge(act.sem, act.at(n_batch + 1))
                eng.activation(key[:, 1:L + 1], key[:, 1:L + 1], ACT.Identity, bias=end_keys[:, 1:2], scale=-1.0
                               ).then_inc(act.sem, 1)
                for j in range(n_batch):
                    t = slice(j * batch, (j + 1) * batch)
                    eng.wait_ge(ve.sem, ve.at(chain_n + (j + 1) * ops))
                    eng.activation(ex[:, t, 0:heads, :], lg[:, t, :, :], ACT.Exp, scale=scale
                                   ).then_inc(act.sem, 1)

            @block.vector
            def _(eng):
                link = Chain(eng, ve)
                eng.memset(open_f[:, 0:1], -BIG)
                eng.memset(open_b[:, R:R + 1], -BIG)
                eng.memset(row[:, 4 * R:4 * R + 1], -BIG)
                if not with_max:
                    eng.memset(extra[:, :].rearrange("p (t c) -> p t c", c=EXTRA)[:, :, heads:EXTRA], 1.0)
                for j in range(n_batch):
                    if j >= 2:
                        eng.wait_ge(pe.sem, pe.at(j - 1))
                    eng.tensor_copy(stage[:, j % 2, :].rearrange("p (t h s) -> p t h s", t=batch, h=heads),
                                    lg[:, j * batch:(j + 1) * batch, :, :]).then_inc(staged.sem, 1)
                eng.wait_ge(dma.sem, dma.at(16 * heads))
                link(eng.tensor_tensor(reset[:, :], key[:, 1:L + 2], key[:, 0:L + 1], ALU.subtract))
                eng.tensor_tensor(ends[:, 2:3], key[:, L:L + 1], key[:, 1:2], ALU.subtract)
                eng.tensor_copy(ends[:, 3:4], reset[:, 0:1])
                eng.tensor_scalar(end_keys[:, 0:1], key[:, 1:2], -1.0, None, ALU.mult)
                eng.tensor_copy(end_keys[:, 1:2], key[:, L:L + 1])
                eng.wait_ge(act.sem, act.at(n_batch))
                link(eng.tensor_tensor_scan(fw[:, :], reset[:, 0:L], lt[:, :], -BIG, ALU.add, ALU.max))
                link(eng.tensor_tensor_scan(backwards(lt[:, :]), backwards(reset[:, 1:L + 1]), backwards(fw[:, :]),
                                            -BIG, ALU.add, ALU.max))
                eng.tensor_copy(ends[:, 0:1], fw[:, L - 1:L])
                link(eng.tensor_copy(ends[:, 1:2], lt[:, 0:1]))
                eng.wait_ge(pe.sem, pe.at(n_batch + 1))
                link(eng.tensor_copy(row[:, 0:4 * R].rearrange("p (c r) -> p c r", c=4),
                                     B.ps[0:1, 0:512].rearrange("p (c r) -> p c r", c=4)[:, :, 0:R]))
                fwd_end, bwd_end, through, going_on = (row[:, c * R:(c + 1) * R] for c in range(4))
                going_on_next = row[:, 3 * R + 1:4 * R + 1]
                link(eng.tensor_tensor(pen[:, 0:R], going_on, through, ALU.add))
                link(eng.tensor_tensor(pen[:, R:2 * R], going_on_next, through, ALU.add))
                link(eng.tensor_tensor_scan(open_f[:, 1:R + 1], pen[:, 0:R], fwd_end, -BIG, ALU.add, ALU.max))
                link(eng.tensor_tensor_scan(backwards(open_b[:, 0:R]), backwards(pen[:, R:2 * R]),
                                            backwards(bwd_end), -BIG, ALU.add, ALU.max))
                link(eng.tensor_tensor(carry_row[:, 0:R], open_f[:, 0:R], going_on, ALU.add))
                link(eng.tensor_tensor(carry_row[:, R:2 * R], open_b[:, 1:R + 1], going_on_next, ALU.add))
                link(eng.tensor_scalar(carry_row[:, :], carry_row[:, :], -BIG, None, ALU.max))
                eng.wait_ge(pe.sem, pe.at(n_batch + 2))
                link(eng.tensor_copy(carry[:, :], B.ps[0:R, 512:514]))
                eng.wait_ge(act.sem, act.at(n_batch + 1))
                link(eng.scalar_tensor_tensor(out=lt[:, :], in0=fw[:, :], scalar=carry[:, 0:1], in1=lt[:, :],
                                              op0=ALU.add, op1=ALU.max))
                eng.wait_ge(act.sem, act.at(n_batch + 2))
                link(eng.scalar_tensor_tensor(out=lt[:, :], in0=key[:, 1:L + 1], scalar=carry[:, 1:2], in1=lt[:, :],
                                              op0=ALU.add, op1=ALU.max))
                assert link.n == chain_n
                last = B.edge_last[:, 0:STEPS].rearrange("p (s t o) -> p t o s", s=slices, o=1)
                for j in range(n_batch):
                    eng.wait_ge(pe.sem, pe.at(n_batch + 3 + j))
                    t = slice(j * batch, (j + 1) * batch)
                    top = B.ps[:, (j % 7) * 512:(j % 7) * 512 + 512].rearrange(
                        "p (t q) -> p t q", q=P)[:, 0:batch, 0:R].rearrange("p t (h s) -> p t h s", h=heads)
                    if with_max:
                        eng.tensor_tensor(ex[:, t, heads:2 * heads, :], top,
                                          last[:, t, :, :].to_broadcast([P, batch, heads, slices]),
                                          ALU.mult).then_inc(ve.sem, 1)
                    eng.tensor_tensor(lg[:, t, :, :], lg[:, t, :, :], top, ALU.subtract).then_inc(ve.sem, 1)
        pe.advance(2 * n_batch + 2)
        act.advance(2 * n_batch + 2)
        ve.advance(chain_n + n_batch * ops)
        dma.advance(16 * heads)
        staged.advance(n_batch)


def value_pass(B, heads, extra, extra_width):
    nc = B.nc
    dim = D // heads
    BF16 = mybir.dt.bfloat16
    with ExitStack() as ctx:
        vals = B.sb(ctx, "vals", [P, BODY_GROUPS, WIDE])
        hot = B.sb(ctx, "vhot", [P, BODY_GROUPS, GROUP, P])
        hot_b = B.sb(ctx, "vhot_b", [P, BODY_GROUPS, GROUP, P], BF16)
        mix = B.sb(ctx, "mix", [P, BODY_GROUPS, WIDE])
        parts = B.sb(ctx, "parts", [P, BODY_GROUPS, GROUP, PART_WIDE], BF16)
        rest = B.sb(ctx, "rest", [P, BODY_GROUPS, GROUP, EXTRA])
        loaded = [B.count(f"loaded{q}") for q in range(BODY_GROUPS)]
        mixed, used, hot_made, halved, split = (B.count(n) for n in ("mixed", "used", "vhot", "halved", "split"))
        blank = B.count("blank")

        def extras_of(n):
            return extra[:, bass.ds(n * (GROUP * EXTRA), GROUP * EXTRA)].rearrange(
                "p (k c) -> p k c", c=EXTRA)[:, :, 0:extra_width]

        def part(q, j):
            return parts[:, q, :, j * EXTRA:j * EXTRA + extra_width]

        with nc.Block() as block:
            @block.sync
            def _(eng):
                with eng.Fori(0, TURNS) as i:
                    for q in range(BODY_GROUPS):
                        n = i * BODY_GROUPS + q
                        eng.wait_ge(mixed.sem, mixed.at(1) + n)
                        eng.dma_start(vals[:, q, :], B.spool[bass.ds(n * P, P), :]).then_inc(loaded[q].sem, 16)

            @block.scalar
            def _(eng):
                eng.wait_ge(blank.sem, blank.at(1))
                with eng.Fori(0, TURNS) as i:
                    for q in range(BODY_GROUPS):
                        n = i * BODY_GROUPS + q
                        eng.wait_ge(used.sem, used.at(1) + n)
                        eng.activation(part(q, 0), extras_of(n), ACT.Copy).then_inc(halved.sem, 1)
                        eng.wait_ge(hot_made.sem, hot_made.at(1) + n)
                        eng.activation(hot_b[:, q, :, :], hot[:, q, :, :], ACT.Copy).then_inc(halved.sem, 1)
                        eng.wait_ge(split.sem, split.at(1) + n * 2)
                        eng.activation(part(q, 1), rest[:, q, :, 0:extra_width], ACT.Copy).then_inc(halved.sem, 1)

            @block.gpsimd
            def _(eng):
                with eng.Fori(0, TURNS) as i:
                    for q in range(BODY_GROUPS):
                        n = i * BODY_GROUPS + q
                        eng.wait_ge(halved.sem, halved.at(1) + n * 3)
                        eng.tensor_tensor(rest[:, q, :, 0:extra_width], extras_of(n), part(q, 0), ALU.subtract
                                          ).then_inc(split.sem, 1)
                        eng.wait_ge(halved.sem, halved.at(3) + n * 3)
                        eng.tensor_tensor(part(q, 2), rest[:, q, :, 0:extra_width], part(q, 1), ALU.subtract
                                          ).then_inc(split.sem, 1)

            @block.vector
            def _(eng):
                eng.memset(B.extra_sums[:, :, :], 1.0)
                eng.memset(parts[:, :, :, :], 0.0).then_inc(blank.sem, 1)
                eng.sem_inc(mixed.sem, BODY_GROUPS)
                with eng.Fori(0, TURNS) as i:
                    for q in range(BODY_GROUPS):
                        n = i * BODY_GROUPS + q
                        eng.wait_ge(used.sem, used.at(1) + n)
                        one_hot(B, eng, hot[:, q, :, :], n * GROUP).then_inc(hot_made.sem, 1)
                        eng.wait_ge(loaded[q].sem, loaded[q].at(16) + i * 16)
                        f = extra[:, bass.ds(n * (GROUP * EXTRA), GROUP * EXTRA)].rearrange(
                            "p (k c) -> p k c", c=EXTRA)[:, :, 0:heads].rearrange(
                            "p k (h o) -> p k h o", o=1).to_broadcast([P, GROUP, heads, dim])
                        eng.tensor_tensor(mix[:, q, :].rearrange("p (k h d) -> p k h d", k=GROUP, h=heads),
                                          vals[:, q, :].rearrange("p (k h d) -> p k h d", k=GROUP, h=heads),
                                          f, ALU.mult).then_inc(mixed.sem, 1)

            @block.tensor
            def _(eng):
                eng.sem_inc(used.sem, BODY_GROUPS)
                clear_sums(B, eng)
                columns = ColumnRegisters(B, eng, with_extras=True)
                with eng.Fori(0, TURNS) as i:
                    sum_at, extra_at = columns.load(i)
                    for q in range(BODY_GROUPS):
                        n = i * BODY_GROUPS + q
                        eng.wait_ge(halved.sem, halved.at(2) + n * 3)
                        eng.wait_ge(split.sem, split.at(2) + n * 2)
                        eng.wait_ge(mixed.sem, mixed.at(BODY_GROUPS + 1) + n)
                        for k in range(GROUP):
                            s = q * GROUP + k
                            eng.matmul(B.ps[:, bass.ds(sum_at[s], D)], hot[:, q, k, :],
                                       mix[:, q, k * D:(k + 1) * D], start=False, stop=True,
                                       skip_group_check=True)
                            ins = eng.matmul(B.ps[:, bass.ds(extra_at[s], PART_WIDE)], hot_b[:, q, k, :], parts[:, q, k, :],
                                             start=False, stop=True, skip_group_check=True)
                        ins.then_inc(used.sem, 1)
                columns.free()
        for c in loaded:
            c.advance(16 * TURNS)
        hot_made.advance(STEP_GROUPS)
        halved.advance(3 * STEP_GROUPS)
        split.advance(2 * STEP_GROUPS)
        blank.advance(1)
        mixed.advance(STEP_GROUPS + BODY_GROUPS)
        used.advance(STEP_GROUPS + BODY_GROUPS)

    work = []
    for at, lo, hi in ((EXTRA_AT, 0, EXTRA_SPLIT), (EXTRA_REST_AT, EXTRA_SPLIT, BLOCKS)):
        low, middle, high = (B.ps[:, at:at + (hi - lo) * PART_COLS].rearrange(
            "p (b j c) -> p b j c", j=PARTS, c=EXTRA)[:, :, j, :] for j in (2, 1, 0))
        sums = B.extra_sums[:, lo:hi, :]
        work += [("vector", lambda e, s=sums, a=low: e.tensor_copy(s, a)),
                 ("vector", lambda e, s=sums, a=middle: e.tensor_tensor(s, s, a, ALU.add)),
                 ("vector", lambda e, s=sums, a=high: e.tensor_tensor(s, s, a, ALU.add))]
    vector_work(B, work)


def vector_work(B, ops):
    done = B.count("small")

    def program(which):
        def run(eng):
            for n, (e, emit) in enumerate(ops):
                if e == which:
                    if n:
                        eng.wait_ge(done.sem, done.at(n))
                    emit(eng).then_inc(done.sem, 1)
        return run
    with B.nc.Block() as block:
        block.vector(program("vector"))
        block.scalar(program("scalar"))
    done.advance(len(ops))


def extras(B, lo, hi):
    return B.extra_sums[:, :, lo:hi]



def attention_layer(B):
    w = {k: B.ins["L0_gnn_" + k] for k in ("Wq", "bq", "Wk", "bk", "Wv", "bv", "Wo", "bo", "ln1_g", "ln1_b",
                                          "W1", "b1", "W2", "b2", "ln2_g", "ln2_b")}
    heads, hidden = 8, 4
    table = B.dram("kv", [NODES_PAD, 2 * D])
    with ExitStack() as ctx:
        inv = B.sb(ctx, "inv", [P, BLOCKS_PAD * heads])
        with ExitStack() as ectx:
            extra = B.sb(ectx, "extra", [P, STEPS * EXTRA])
            with ExitStack() as lctx:
                logits = B.sb(lctx, "logits", [P, STEPS * heads])
                with ExitStack() as pctx:
                    q = B.sb(pctx, "q", [P, GROUPS * WIDE])
                    with ExitStack() as kctx:
                        k_, v_, xt = (B.sb(kctx, n, [P, GROUPS * WIDE]) for n in ("k", "v", "xt"))
                        wt = {n: B.sb(kctx, n, [P, D]) for n in ("Wq", "Wk", "Wv", "bq", "bk", "bv")}
                        load(B, [(wt[n][:, :], w[n]) for n in ("Wq", "Wk", "Wv")]
                             + [(wt[n][:, :], rows_of(w[n], D)) for n in ("bq", "bk", "bv")])
                        steps = transpose_steps(B, "xt", B.x, xt, [])
                        before = "xt"
                        for dst, c in ((q, "q"), (k_, "k"), (v_, "v")):
                            steps.append(matmul_step(c + "mm", B, [(xt, wt["W" + c][:, :])], [before]))
                            steps.append(add_row_step(c, dst, B.ps, wt["b" + c], ALU.add, [c + "mm"]))
                            before = c
                        steps += [store_step("store_k", table, 0, k_, ["k"]), store_step("store_v", table, D, v_, ["v"])]
                        node_sweeps(B, steps)
                    score_pass(B, table, 2 * D, heads, q, None, logits)
                segment_softmax(B, heads, 1.0 / (D // heads) ** 0.5, logits, extra, False)
            value_pass(B, heads, extra, heads + 1)
        vector_work(B, [
            ("vector", lambda e: e.tensor_copy(B.degree[:, :].rearrange("p (b o) -> p b o", o=1), extras(B, heads, heads + 1))),
            ("vector", lambda e: e.tensor_scalar(inv[:, :].rearrange("p (b h) -> p b h", h=heads), extras(B, 0, heads),
                                                 1e-16, None, ALU.add)),
            ("vector", lambda e: e.reciprocal(inv[:, :], inv[:, :])),
            ("vector", lambda e: e.tensor_scalar(B.degree_1[:, :], B.degree[:, :], 1.0, None, ALU.add)),
            ("vector", lambda e: e.reciprocal(B.inv_degree[:, :], B.degree_1[:, :])),
            ("scalar", lambda e: e.activation(B.root_degree[:, :], B.degree_1[:, :], ACT.Sqrt)),
            ("vector", lambda e: e.reciprocal(B.root_degree[:, :], B.root_degree[:, :])),
        ])
        agg, tr = (B.sb(ctx, n, [P, GROUPS * WIDE]) for n in ("agg", "tr"))
        h1 = [B.sb(ctx, f"h1_{c}", [P, GROUPS * WIDE]) for c in range(hidden)]
        wo = B.sb(ctx, "wo", [P, D])
        w1 = B.sb(ctx, "w1", [P, hidden * D])
        w2 = B.sb(ctx, "w2", [P, hidden, D])
        b1 = B.sb(ctx, "b1", [P, hidden])
        vec = {n: B.sb(ctx, n, [P, D]) for n in ("bo", "b2", "ln1_g", "ln1_b", "ln2_g", "ln2_b")}
        load(B, [(wo[:, :], w["Wo"]), (w1[:, :], w["W1"]), (w2[:, :, :], w["W2"].rearrange("(c p) d -> p c d", p=P)),
                 (b1[:, :], w["b1"].rearrange("(c p) -> p c", p=P))] + [(vec[n][:, :], rows_of(w[n], D)) for n in vec])

        def hidden_mm(c):
            return lambda eng, g: eng.matmul(B.bank(g), w1[:, c * D:(c + 1) * D],
                                             tr[:, g * WIDE:(g + 1) * WIDE], start=True, stop=True)

        def hidden_relu(c):
            return lambda eng, g: eng.activation(grp(h1[c], g), grp(B.ps, g), ACT.Relu, bias=b1[:, c:c + 1])
        steps = [scale_heads_step("agg", agg, B.ps, inv, heads, [])]
        steps += transpose_steps(B, "aggt", agg, tr, ["agg"])
        steps += [matmul_step("out", B, [(tr, wo[:, :])], ["aggt"]),
                  add_row_step("out_b", agg, B.ps, vec["bo"], ALU.add, ["out"]),
                  add_step("res1", agg, agg, B.x, ["out_b"])]
        steps += layernorm_steps(B, "ln1", agg, agg, ["res1"], vec["ln1_g"], vec["ln1_b"])
        steps += transpose_steps(B, "ht", agg, tr, ["ln1"])
        before = "ht"
        for c in range(hidden):
            steps += [(f"ff{c}", "tensor", [before], hidden_mm(c)),
                      (f"relu{c}", "scalar", [f"ff{c}"], hidden_relu(c))]
            before = f"relu{c}"
        steps += [matmul_step("ff", B, [(h1[c], w2[:, c, :]) for c in range(hidden)], [before]),
                  add_row_step("ff_b", tr, B.ps, vec["b2"], ALU.add, ["ff"]),
                  add_step("res2", agg, agg, tr, ["ff_b"])]
        steps += layernorm_steps(B, "ln2", agg, agg, ["res2"], vec["ln2_g"], vec["ln2_b"])
        steps += [add_step("res3", B.x, B.x, agg, ["ln2"])]
        steps += layernorm_steps(B, "x", B.x, B.x, ["res3"])
        steps += [store_step("store", B.gcn_table, 0, B.x, ["x"])]
        node_sweeps(B, steps)


def gcn_layers(B):
    ins = B.ins
    layers = 2
    table = B.gcn_table
    with ExitStack() as ctx:
        h, agg, tr, trx = (B.sb(ctx, n, [P, GROUPS * WIDE]) for n in ("h", "gagg", "gtr", "gtrx"))
        raw = {k: B.sb(ctx, k, [P, D]) for k in ("self0", "self1", "neigh0", "neigh1", "out")}
        wt = {k: B.sb(ctx, k + "_t", [P, D]) for k in raw}
        bias = {l: [B.sb(ctx, f"bias{l}{j}", [P, D]) for j in range(3)] for l in range(layers)}
        b_out = B.sb(ctx, "b_out", [P, D])
        load(B, [(raw["self0"][:, :], ins["L1_gnn_W_self"][0]), (raw["self1"][:, :], ins["L1_gnn_W_self"][1]),
                 (raw["neigh0"][:, :], ins["L1_gnn_W_neigh"][0]), (raw["neigh1"][:, :], ins["L1_gnn_W_neigh"][1]),
                 (raw["out"][:, :], ins["L1_gnn_W_agg"]), (b_out[:, :], rows_of(ins["L1_gnn_b_agg"], D))]
             + [(bias[l][j][:, :], rows_of(ins["L1_gnn_" + n][l], D))
                for l in range(layers) for j, n in enumerate(("b_self", "b_neigh", "layer_bias"))])
        turn_weights(B, [(wt[k][:, :], raw[k][:, :]) for k in raw])
        vector_work(B, [("vector", lambda e, l=l, j=j: e.tensor_tensor(bias[l][0][:, :], bias[l][0][:, :],
                                                                       bias[l][j][:, :], ALU.add))
                        for l in range(layers) for j in (1, 2)])
        cur = B.x
        for l in range(layers):
            gcn_pass(B, table)
            steps = [add_step("sum", agg, B.ps, cur, []),
                     scale_heads_step("mean", agg, agg, B.inv_degree, 1, ["sum"])]
            steps += transpose_steps(B, "aggt", agg, tr, ["mean"])
            steps += transpose_steps(B, "xt", cur, trx, ["aggt"])
            steps += [matmul_step("mm", B, [(trx, wt[f"self{l}"][:, :]), (tr, wt[f"neigh{l}"][:, :])], ["aggt", "xt"]),
                      add_row_step("pre", agg, B.ps, bias[l][0], ALU.add, ["mm"]),
                      leaky_step("h", h, agg, ["pre"])]
            if l < layers - 1:
                steps += [store_step("store", table, 0, h, ["h"])]
            else:
                steps += transpose_steps(B, "ht", h, tr, ["h"])
                steps += [matmul_step("mm2", B, [(tr, wt["out"][:, :])], ["ht"]),
                          add_row_step("o", agg, B.ps, b_out, ALU.add, ["mm2"]),
                          add_step("res", B.x, B.x, agg, ["o"])]
                steps += layernorm_steps(B, "x", B.x, B.x, ["res"])
            node_sweeps(B, steps)
            cur = h


def gatv2_layers(B):
    table = B.dram("gat", [NODES_PAD, D])
    with ExitStack() as ctx:
        h, xl, xr = (B.sb(ctx, n, [P, GROUPS * WIDE]) for n in ("gh", "xl", "xr"))
        weights = {layer: {n: B.sb(ctx, f"gat{layer}_{n}", [P, D]) for n in ("Wl", "Wr", "bl", "br", "a", "c", "g", "be")}
                   for layer in (1, 2, 3)}
        pairs = []
        for layer, wt in weights.items():
            for n, tile in wt.items():
                w = B.ins[f"L2_gnn_{n[0]}{layer}{n[1:]}" if n in ("Wl", "Wr", "bl", "br") else f"L2_gnn_{n}{layer}"]
                pairs.append((tile[:, :], w if n in ("Wl", "Wr") else rows_of(w, D)))
        load(B, pairs)
        for layer, heads in ((1, 4), (2, 4), (3, 1)):
            wt = weights[layer]
            cur = B.x if layer == 1 else h
            with ExitStack() as lctx:
                own = B.sb(lctx, "own", [P, BLOCKS_PAD * heads])
                with ExitStack() as tctx:
                    tr, z = (B.sb(tctx, n, [P, GROUPS * WIDE]) for n in ("gat_tr", "gat_z"))
                    steps = transpose_steps(B, "xt", cur, tr, [])
                    steps += [matmul_step("lmm", B, [(tr, wt["Wl"][:, :])], ["xt"]),
                              add_row_step("l", xl, B.ps, wt["bl"], ALU.add, ["lmm"]),
                              matmul_step("rmm", B, [(tr, wt["Wr"][:, :])], ["l"]),
                              add_row_step("r", xr, B.ps, wt["br"], ALU.add, ["rmm"]),
                              add_step("z", z, xl, xr, ["r"]),
                              leaky_step("lz", z, z, ["z"]),
                              add_row_step("az", z, z, wt["a"], ALU.mult, ["lz"]),
                              ("own", "vector", ["az"], lambda eng, g: eng.tensor_reduce(
                                  grp(own, g, GROUP * heads), grp(z, g).rearrange("p (m d) -> p m d", d=D // heads),
                                  X_AXIS, ALU.add))]
                    steps += [store_step("store", table, 0, xl, ["l"])]
                    node_sweeps(B, steps)
                with ExitStack() as ectx:
                    extra = B.sb(ectx, "gextra", [P, STEPS * EXTRA])
                    with ExitStack() as sctx:
                        logits = B.sb(sctx, "glogits", [P, STEPS * heads])
                        score_pass(B, table, D, heads, xr, wt["a"], logits)
                        segment_softmax(B, heads, 1.0, logits, extra, True)
                    value_pass(B, heads, extra, 2 * heads)
                top, tot, new, we, ws = (B.sb(lctx, n, [P, BLOCKS_PAD * heads]) for n in ("top", "tot", "new", "we", "ws"))
                none = B.sb(lctx, "none", [P, BLOCKS_PAD])

                def by_node(t):
                    return t[:, :].rearrange("p (b h) -> p b h", h=heads)

                def vv(dst, a, b, op):
                    return ("vector", lambda e: e.tensor_tensor(dst, a, b, op))
                vector_work(B, [
                    ("vector", lambda e: e.tensor_scalar(none[:, :], B.degree[:, :], 0.5, -BIG, ALU.is_lt, ALU.mult)),
                    vv(by_node(top), extras(B, heads, 2 * heads), none[:, :].rearrange("p (b o) -> p b o", o=1)
                       .to_broadcast([P, BLOCKS_PAD, heads]), ALU.add),
                    vv(new[:, :], top[:, :], own[:, :], ALU.max),
                    vv(we[:, :], top[:, :], new[:, :], ALU.subtract),
                    vv(ws[:, :], own[:, :], new[:, :], ALU.subtract),
                    ("scalar", lambda e: e.activation(we[:, :], we[:, :], ACT.Exp)),
                    ("scalar", lambda e: e.activation(ws[:, :], ws[:, :], ACT.Exp)),
                    vv(by_node(tot), extras(B, 0, heads), by_node(we), ALU.mult),
                    vv(tot[:, :], tot[:, :], ws[:, :], ALU.add),
                    ("vector", lambda e: e.reciprocal(tot[:, :], tot[:, :])),
                    vv(we[:, :], we[:, :], tot[:, :], ALU.mult),
                    vv(ws[:, :], ws[:, :], tot[:, :], ALU.mult),
                ])
                steps = [scale_heads_step("e", h, B.ps, we, heads, []),
                         scale_heads_step("s", xl, xl, ws, heads, []),
                         add_step("sum", h, h, xl, ["e", "s"]),
                         add_row_step("c", h, h, wt["c"], ALU.add, ["sum"])]
                steps += layernorm_steps(B, "ln", h, h, ["c"], wt["g"], wt["be"])
                steps += [("h", "scalar", ["ln"], lambda eng, g: eng.activation(grp(h, g), grp(h, g), ACT.Relu))]
                if layer == 3:
                    steps += [add_step("res", B.x, B.x, h, ["h"])]
                    steps += layernorm_steps(B, "x", B.x, B.x, ["res"])
                node_sweeps(B, steps)


def normalised_gcn_layer(B):
    table = B.dram("norm", [NODES_PAD, D])
    ins = B.ins
    with ExitStack() as ctx:
        a, tr = (B.sb(ctx, n, [P, GROUPS * WIDE]) for n in ("na", "ntr"))
        wt = {n: B.sb(ctx, "n_" + n, [P, D]) for n in ("W", "b", "gamma", "beta")}
        load(B, [(wt["W"][:, :], ins["L3_gnn_W"])]
             + [(wt[n][:, :], rows_of(ins["L3_gnn_" + n], D)) for n in ("b", "gamma", "beta")])
        node_sweeps(B, [scale_heads_step("s", a, B.x, B.root_degree, 1, []), store_step("store", table, 0, a, ["s"])])
        gcn_pass(B, table)
        steps = [scale_heads_step("s", a, B.ps, B.root_degree, 1, []),
                 add_step("sum", a, a, B.x, ["s"])]
        steps += transpose_steps(B, "t", a, tr, ["sum"])
        steps += [matmul_step("mm", B, [(tr, wt["W"][:, :])], ["t"]),
                  add_row_step("b", a, B.ps, wt["b"], ALU.add, ["mm"]),
                  ("gelu", "scalar", ["b"], lambda eng, g: eng.activation(grp(a, g), grp(a, g), ACT.Gelu))]
        steps += layernorm_steps(B, "ln", a, a, ["gelu"], wt["gamma"], wt["beta"])
        steps += [add_step("res", a, a, B.x, ["ln"])]
        steps += layernorm_steps(B, "x", B.x, a, ["res"])
        node_sweeps(B, steps)
    store(B, [(B.out[0:FULL_BLOCKS * P, :].rearrange("(b p) d -> p b d", p=P), over_groups(B.x[:, 0:FULL_BLOCKS * D])),
              (B.out[FULL_BLOCKS * P:N_NODES, :], B.x[0:LAST_NODES, FULL_BLOCKS * D:(FULL_BLOCKS + 1) * D])])


def build(nc, ins, out):
    with ExitStack() as ctx:
        B = Builder(nc, ctx, ins, out)
        B.ps = ctx.enter_context(nc.psum_tensor("sums", [P, 8 * 512], F32))
        B.x = B.sb(ctx, "x", [P, GROUPS * WIDE])
        B.ident = B.sb(ctx, "ident", [P, P])
        B.zeros = B.sb(ctx, "zeros", [P, 512], mybir.dt.bfloat16)
        B.iota = B.sb(ctx, "iota", [P, P])
        B.eps = B.sb(ctx, "eps", [P, 1])
        B.edge_src, B.edge_local, B.edge_weight, B.edge_last = (
            B.sb(ctx, n, [P, STEPS_PAD]) for n in ("edge_src", "edge_local", "edge_weight", "edge_last"))
        B.index_ring = B.sb(ctx, "index_ring", [P, BODY], I32)
        B.columns = B.sb(ctx, "columns", [1, STEPS * 2], mybir.dt.uint16)
        B.ln_stats = B.sb(ctx, "ln_stats", [P, BLOCKS_PAD * 6])
        B.ln_mean_var = B.sb(ctx, "ln_mean_var", [P, BLOCKS_PAD * 2])
        B.ln_rstd = B.sb(ctx, "ln_rstd", [P, BLOCKS_PAD])
        B.degree, B.degree_1, B.inv_degree, B.root_degree = (
            B.sb(ctx, n, [P, BLOCKS_PAD]) for n in ("degree", "degree_1", "inv_degree", "root_degree"))
        B.extra_sums = B.sb(ctx, "extra_sums", [P, BLOCKS_PAD, EXTRA])
        B.spool = B.dram("spool", [STEP_GROUPS * P, WIDE])
        B.gcn_table = B.dram("gcn", [NODES_PAD, D])
        lay_out_edges(B)
        attention_layer(B)
        gcn_layers(B)
        gatv2_layers(B)
        normalised_gcn_layer(B)


def kernel(**inputs):
    import numpy as np
    import concourse.bacc as bacc
    from concourse.bass_utils import run_bass_kernel_spmd

    nc = bacc.Bacc("TRN2", target_bir_lowering=False, num_devices=1)
    arrays, handles = {}, {}
    for name, value in inputs.items():
        a = np.ascontiguousarray(value)
        arrays["in_" + name] = a
        handles[name] = nc.dram_tensor("in_" + name, a.shape, mybir.dt.from_np(a.dtype), kind="ExternalInput").ap()
    out = nc.dram_tensor("out", (N_NODES, D), F32, kind="ExternalOutput").ap()
    build(nc, handles, out)
    result = run_bass_kernel_spmd(nc, [arrays], core_ids=[0])
    return result.results[0]["out"]
```
